# Optimizing a Trainium2 kernel written in Bass

```python
import numpy as np
import jax
import jax.numpy as jnp

def _softmax(x, axis=-1):
    return jax.nn.softmax(x, axis=axis)

def _gelu(x):
    return jax.nn.gelu(x, approximate=True)

def _silu(x):
    return jax.nn.silu(x)

def _sigmoid(x):
    return jax.nn.sigmoid(x)

def _layernorm(x, axis=-1, eps=1e-05):
    m = jnp.mean(x, axis=axis, keepdims=True)
    v = jnp.var(x, axis=axis, keepdims=True)
    return (x - m) / jnp.sqrt(v + eps)

def _scatter_add(tgt, idx, src, axis=0):
    return tgt.at[idx].add(src)

def _segment_sum(src, seg, n):
    return jax.ops.segment_sum(src, seg, n)
kernel_name = 'mk_xattn_ffn_d1_seqx_r4_51889e'

def setup_inputs(seed: int=0):
    np.random.seed(seed)
    _w = jnp.asarray

    def _rec_inputs():
        import jax
        import jax.numpy as jnp
        _rk = jax.random.key(seed)
        x = 7.22e-05 + 1 * jax.random.normal(jax.random.fold_in(_rk, 1), (16, 128, 512), jnp.float32)
        _lenS = 128 - jax.random.randint(jax.random.fold_in(_rk, 7), (16,), 0, max(1, 128 // 4) + 1, jnp.int32)
        _lenS2 = 128 - jax.random.randint(jax.random.fold_in(_rk, 8), (16,), 0, max(1, 128 // 4) + 1, jnp.int32)
        _ctx_2048P = jax.random.normal(jax.random.fold_in(_rk, 11), (16, 16, 512), jnp.float32)
        _ctx_2048c = jax.random.dirichlet(jax.random.fold_in(_rk, 511), 0.3 * jnp.ones((16,), jnp.float32), (16, 128))
        _ctx_2048t = jnp.einsum('bsk,bkd->bsd', _ctx_2048c, _ctx_2048P)
        _ctx_2048t = _ctx_2048t * jax.lax.rsqrt(jnp.mean(jnp.square(_ctx_2048t)) + 1e-12) * 0.953939
        ctx_2048 = 4.13588e-05 + 0.999923 * (_ctx_2048t + 0.3 * jax.random.normal(jax.random.fold_in(_rk, 611), (16, 128, 512), jnp.float32))
        return (x, ctx_2048)
    x, ctx_2048 = _rec_inputs()

    def _L0_xattn_setup():
        import jax, jax.numpy as jnp
        import numpy as np
        B, S, DIM, HD = (4, 256, 512, 128)
        H = DIM // HD
        GN_EPS = 0.001

        def _decay_masks(n_heads, seq_len):
            gam = 1.0 - 2.0 ** (-5.0 - jnp.arange(n_heads, dtype=jnp.float32))
            idx = jnp.arange(seq_len, dtype=jnp.float32)
            expo = idx[None, :] - idx[:, None]
            D = jnp.where(expo[None, :, :] <= 0, gam[:, None, None] ** expo[None, :, :], 0.0)
            return D / jnp.sqrt(D.sum(axis=-1))[:, None, :]
        key = jax.random.key(seed)
        ks = jax.random.split(key, 8)
        x = jax.random.normal(ks[0], (B, S, DIM), dtype=jnp.float32)
        k = jax.random.normal(ks[1], (B, S, DIM), dtype=jnp.float32)
        v = jax.random.normal(ks[2], (B, S, DIM), dtype=jnp.float32)
        Wh = jax.random.normal(ks[3], (H, HD, HD), dtype=jnp.float32) / np.sqrt(HD)
        wg_w = jax.random.normal(ks[4], (DIM, DIM), dtype=jnp.float32) / np.sqrt(DIM)
        wo_w = jax.random.normal(ks[5], (DIM, DIM), dtype=jnp.float32) / np.sqrt(DIM)
        gn_gamma = jnp.ones((DIM,), dtype=jnp.float32)
        gn_beta = jnp.zeros((DIM,), dtype=jnp.float32)
        return {'x': x, 'k': k, 'v': v, 'Wh': Wh, 'wg_w': wg_w, 'wo_w': wo_w, 'gn_gamma': gn_gamma, 'gn_beta': gn_beta}
    _L0_xattn_all = _L0_xattn_setup()
    _L0_xattn_in = {k: v for k, v in _L0_xattn_all.items() if k in ('Wh', 'wg_w', 'wo_w', 'gn_gamma', 'gn_beta')}
    del _L0_xattn_all

    def _L0_ffn_setup():
        import jax, jax.numpy as jnp
        import numpy as np
        DIM = 512
        EXPERT_DIM = 256
        N_EXPERTS = 16
        TOPK = 2
        N_SHARED = 1
        B, T = (4, 512)
        key = jax.random.key(seed)
        ks = jax.random.split(key, 9)
        s = 0.02
        return {'x': jax.random.normal(ks[0], (B, T, DIM), jnp.float32), 'router_w': jax.random.normal(ks[1], (N_EXPERTS, DIM), jnp.float32) * s, 'router_bias': jnp.zeros((N_EXPERTS,), jnp.float32), 'Wu': jax.random.normal(ks[2], (N_EXPERTS, DIM, EXPERT_DIM), jnp.float32) * s, 'Wg': jax.random.normal(ks[3], (N_EXPERTS, DIM, EXPERT_DIM), jnp.float32) * s, 'Wd': jax.random.normal(ks[4], (N_EXPERTS, EXPERT_DIM, DIM), jnp.float32) * s, 'Su': jax.random.normal(ks[5], (N_SHARED, DIM, EXPERT_DIM * TOPK), jnp.float32) * s, 'Sg': jax.random.normal(ks[6], (N_SHARED, DIM, EXPERT_DIM * TOPK), jnp.float32) * s, 'Sd': jax.random.normal(ks[7], (N_SHARED, EXPERT_DIM * TOPK, DIM), jnp.float32) * s}
    _L0_ffn_all = _L0_ffn_setup()
    _L0_ffn_in = {k: v for k, v in _L0_ffn_all.items() if k in ('router_w', 'router_bias', 'Wu', 'Wg', 'Wd', 'Su', 'Sg', 'Sd')}
    del _L0_ffn_all
    return {'x': x, 'ctx_2048': ctx_2048, 'L0_xattn_Wh': _L0_xattn_in['Wh'], 'L0_xattn_wg_w': _L0_xattn_in['wg_w'], 'L0_xattn_wo_w': _L0_xattn_in['wo_w'], 'L0_xattn_gn_gamma': _L0_xattn_in['gn_gamma'], 'L0_xattn_gn_beta': _L0_xattn_in['gn_beta'], 'L0_ffn_router_w': _L0_ffn_in['router_w'], 'L0_ffn_router_bias': _L0_ffn_in['router_bias'], 'L0_ffn_Wu': _L0_ffn_in['Wu'], 'L0_ffn_Wg': _L0_ffn_in['Wg'], 'L0_ffn_Wd': _L0_ffn_in['Wd'], 'L0_ffn_Su': _L0_ffn_in['Su'], 'L0_ffn_Sg': _L0_ffn_in['Sg'], 'L0_ffn_Sd': _L0_ffn_in['Sd']}

def reference(x, ctx_2048, L0_xattn_Wh, L0_xattn_wg_w, L0_xattn_wo_w, L0_xattn_gn_gamma, L0_xattn_gn_beta, L0_ffn_router_w, L0_ffn_router_bias, L0_ffn_Wu, L0_ffn_Wg, L0_ffn_Wd, L0_ffn_Su, L0_ffn_Sg, L0_ffn_Sd):
    import jax
    import jax.numpy as jnp

    def _L0_xattn_ref(x, k, v, Wh, wg_w, wo_w, gn_gamma, gn_beta):
        import jax, jax.numpy as jnp
        import numpy as np
        B, S, DIM, HD = (4, 256, 512, 128)
        H = DIM // HD
        GN_EPS = 0.001

        def _decay_masks(n_heads, seq_len):
            gam = 1.0 - 2.0 ** (-5.0 - jnp.arange(n_heads, dtype=jnp.float32))
            idx = jnp.arange(seq_len, dtype=jnp.float32)
            expo = idx[None, :] - idx[:, None]
            D = jnp.where(expo[None, :, :] <= 0, gam[:, None, None] ** expo[None, :, :], 0.0)
            return D / jnp.sqrt(D.sum(axis=-1))[:, None, :]
        b, s, dim = x.shape
        h, hd, _ = Wh.shape
        xh = x.reshape(b, s, h, hd)
        kh = k.reshape(b, s, h, hd)
        vh = v.reshape(b, s, h, hd)
        Q = jnp.einsum('bshd,hde->bshe', xh, Wh)
        K = jnp.einsum('bshd,hde->bshe', kh, Wh)
        V = jnp.einsum('bshd,hde->bshe', vh, Wh)
        scores = jnp.einsum('bshe,bthe->bhst', Q, K) / jnp.sqrt(jnp.float32(hd))
        Dn = _decay_masks(h, s)
        masked = scores * Dn[None, :, :, :]
        A = jnp.maximum(jnp.abs(masked.sum(axis=0)), 1.0)
        O = jnp.einsum('hst,bthe->bshe', A, V).reshape(b, s, dim)
        mu = O.mean(axis=-1, keepdims=True)
        var = O.var(axis=-1, keepdims=True)
        Y = (O - mu) / jnp.sqrt(var + GN_EPS) * gn_gamma + gn_beta
        W = jax.nn.relu(x @ wg_w)
        return W * Y @ wo_w

    def _L0_ffn_ref(x, router_w, router_bias, Wu, Wg, Wd, Su, Sg, Sd):
        import jax, jax.numpy as jnp
        import numpy as np
        DIM = 512
        EXPERT_DIM = 256
        N_EXPERTS = 16
        TOPK = 2
        N_SHARED = 1
        B, T = (4, 512)
        Bx, Tx, D = x.shape
        flat = x.reshape(Bx * Tx, D)
        logits = flat @ router_w.T
        scores = jax.nn.softmax(logits, axis=-1)
        _, topk_idx = jax.lax.top_k(logits + router_bias, TOPK)
        topk_scores = jnp.take_along_axis(scores, topk_idx, axis=-1)
        topk_scores = topk_scores / topk_scores.sum(-1, keepdims=True)
        combine = jnp.einsum('nk,nke->ne', topk_scores, jax.nn.one_hot(topk_idx, N_EXPERTS, dtype=scores.dtype))
        out = jnp.zeros_like(flat)
        for e in range(N_EXPERTS):
            h = jax.nn.silu(flat @ Wu[e]) * (flat @ Wg[e])
            out = out + combine[:, e:e + 1] * (h @ Wd[e])
        for s in range(N_SHARED):
            out = out + jax.nn.silu(flat @ Su[s]) * (flat @ Sg[s]) @ Sd[s]
        return out.reshape(Bx, Tx, D)
    x = x + _L0_xattn_ref(_layernorm(x, axis=-1), ctx_2048, ctx_2048, L0_xattn_Wh, L0_xattn_wg_w, L0_xattn_wo_w, L0_xattn_gn_gamma, L0_xattn_gn_beta)
    x = x + _L0_ffn_ref(_layernorm(x, axis=-1), L0_ffn_router_w, L0_ffn_router_bias, L0_ffn_Wu, L0_ffn_Wg, L0_ffn_Wd, L0_ffn_Su, L0_ffn_Sg, L0_ffn_Sd)
    return x

_drawn_inputs = setup_inputs


def setup_inputs(seed=0):
    import zlib

    import numpy as np

    out = dict(_drawn_inputs(seed))
    spreads = {'L0_xattn_gn_gamma': (1.0, 0.2),
     'L0_xattn_gn_beta': (0.0, 0.1),
     'L0_ffn_router_bias': (0.0, 0.8)}
    factors = {'L0_ffn_router_w': 3.015, 'L0_ffn_Wu': 2.87, 'L0_ffn_Wg': 2.807, 'L0_ffn_Wd': 2.802}
    for name, (base, spread) in spreads.items():
        noise = np.random.default_rng([zlib.crc32(name.encode()), seed]).standard_normal(out[name].shape)
        drawn = base * np.exp(spread * noise) if base else spread * noise
        out[name] = jnp.asarray(drawn.astype(out[name].dtype))
    for name, factor in factors.items():
        out[name] = (out[name] * factor).astype(out[name].dtype)
    return out
```

```python
import numpy as np
from contextlib import ExitStack

import concourse.bass as bass
from concourse import mybir

F32 = mybir.dt.float32
F32R = mybir.dt.float32r
BF16 = mybir.dt.bfloat16
I32 = mybir.dt.int32
U32 = mybir.dt.uint32
ALU = mybir.AluOpType
ACT = mybir.ActivationFunctionType
AX = mybir.AxisListType

P = 128
D = 512
C = D // P
NT = 16
GT = 4
NG = NT // GT
GW = GT * P
E = 16
FE = 256
FC = FE // P
TOPK = 2
ROUTED = (NT * P * TOPK + E * (P - 1)) // P
NSLOT = 4
PIECE = 1024
LN_EPS = 1e-5
GN_EPS = 1e-3


def decay_over_root(heads, s, hd):
    gam = (1.0 - 2.0 ** (-5.0 - np.arange(heads, dtype=np.float32))).astype(np.float32)
    expo = np.arange(s, dtype=np.float32)[None, :] - np.arange(s, dtype=np.float32)[:, None]
    d = np.where(expo[None] <= 0, gam[:, None, None] ** expo[None], np.float32(0.0)).astype(np.float32)
    d = d / np.sqrt(d.sum(axis=-1))[:, None, :]
    return np.ascontiguousarray(d.transpose(2, 0, 1) / np.float32(np.sqrt(hd))).astype(np.float32)


def xattn_moe(nc, x, ctx, wh, wg, wo, gamma, beta, rw, rb, Wu, Wg, Wd, Su, Sg, Sd,
              ident_c, decay_c, before_c, ramp_c, out):
    K = 1024
    xn_dram = nc.dram_tensor("xn_rows", [NT, P, D], F32, kind="Internal").ap()
    xs_dram = nc.dram_tensor("sorted_rows", [(ROUTED + 1) * P, D], F32, kind="Internal").ap()
    ys_dram = nc.dram_tensor("expert_rows", [ROUTED * P, D], F32, kind="Internal").ap()

    room = -(-nc.sbuf_base // 32) * 32

    def sb(name, at, shape, dt=F32):
        return nc.alloc_sbuf_tensor_at(name, [shape[0], int(np.prod(shape[1:]))], dt, offset=room + at)[:, :]

    def view(ap, *dims):
        names = "abcd"[:len(dims)]
        return ap.rearrange(f"p ({' '.join(names)}) -> p {' '.join(names)}", **dict(zip(names, dims)))

    def tensor(name, at, dims, dt=F32, parts=P):
        return view(sb(name, at, [parts, *dims], dt), *dims) if len(dims) > 1 else sb(name, at, [parts, *dims], dt)

    x1 = tensor("x1", 0, [NT, D])
    xhT_hi = tensor("xhT_hi", 0, [C, GW], F32R)
    xhT_lo = tensor("xhT_lo", 8 * K, [C, GW], F32R)
    qT = tensor("qT", 16 * K, [C, GW])
    ctxT = tensor("ctxT", 24 * K, [GT, C, P])
    gate = tensor("gateT", 32 * K, [NG, C, GW])
    x2T = tensor("x2T", 32 * K, [NG, C, GW])
    vals = tensor("values", 64 * K, [C, NT, P])
    wo_hi = tensor("wo_hi", 96 * K, [C, D], F32R)
    wo_lo = tensor("wo_lo", 104 * K, [C, D], F32R)
    wg_hi = tensor("wg_hi", 112 * K, [C, D], F32R)
    wg_lo = tensor("wg_lo", 120 * K, [C, D], F32R)
    sd_hi = tensor("sd_hi", 112 * K, [C, D], F32R)
    sd_lo = tensor("sd_lo", 120 * K, [C, D], F32R)
    su_hi = tensor("su_hi", 128 * K, [C, D], F32R)
    su_lo = tensor("su_lo", 136 * K, [C, D], F32R)
    sg_hi = tensor("sg_hi", 144 * K, [C, D], F32R)
    sg_lo = tensor("sg_lo", 152 * K, [C, D], F32R)
    wh_sb = tensor("wh_sb", 144 * K, [C, P])
    whT = tensor("whT", 146 * K, [C, P])
    gram_hi = tensor("gram_hi", 148 * K, [C, P], F32R)
    gram_lo = tensor("gram_lo", 150 * K, [C, P], F32R)
    decay = tensor("decay", 152 * K, [C, P])
    ring_hi = tensor("ring_hi", 64 * K, [NSLOT, 6, PIECE], F32R)
    xin = tensor("xin", 160 * K, [GT, D])
    cin = tensor("cin", 168 * K, [GT, D])
    zeros = tensor("zeros", 176 * K, [D])
    before_f = tensor("before_f", 178 * K, [P])
    yn = tensor("yn", 160 * K, [GT, D])
    mT_hi = tensor("mT_hi", 168 * K, [C, GW], F32R)
    mT_lo = tensor("mT_lo", 176 * K, [C, GW], F32R)
    ya = tensor("ya", 176 * K, [C, GW])
    HW = GW // 2
    sx_hi = tensor("sx_hi", 160 * K, [C, HW], F32R)
    sx_lo = tensor("sx_lo", 164 * K, [C, HW], F32R)
    shT_hi = tensor("shT_hi", 168 * K, [C, HW], F32R)
    shT_lo = tensor("shT_lo", 172 * K, [C, HW], F32R)
    s_silu = tensor("s_silu", 176 * K, [2, HW])
    s_prod = tensor("s_prod", 178 * K, [2, HW])
    oh = tensor("oh", 180 * K, [TOPK, NT, E])
    expl = tensor("expl", 182 * K, [NT, E])
    rank = tensor("rank", 183 * K, [NT, E])
    tmp = tensor("tmp", 184 * K, [NT, E])
    top8 = tensor("top8", 185 * K, [NT, 8])
    top8i = tensor("top8i", 185 * K + 512, [NT, 8], U32)
    lgT = tensor("lgT", 184 * K, [GW], parts=E)
    raw = tensor("raw", 186 * K, [2, PIECE])
    ident = tensor("ident", 194 * K, [P])
    xn = tensor("xn", 194 * K + 512, [GT, D])
    stage = tensor("stage", 194 * K + 512, [GT, D])
    scores = tensor("scores", 202 * K + 512, [C, P])
    tcmp = tensor("tcmp", 202 * K + 512, [ROUTED, E], BF16, parts=1)
    logits = tensor("logits", 204 * K + 512, [NT, E])
    tab_f = tensor("tab_f", 204 * K + 512, [ROUTED], parts=1)
    tab_e = tensor("tab_e", 204 * K + 704, [ROUTED], I32, parts=1)
    tab_s = tensor("tab_s", 204 * K + 896, [ROUTED], I32, parts=1)
    ends_i = tensor("ends_i", 205 * K + 64, [E], I32, parts=1)
    xs = tensor("xs", 32 * K, [4, D])
    xsT_hi = tensor("xsT_hi", 40 * K, [2, C, P], F32R)
    xsT_lo = tensor("xsT_lo", 44 * K, [2, C, P], F32R)
    r_silu = tensor("r_silu", 48 * K, [2, FE])
    r_prod = tensor("r_prod", 50 * K, [2, FE])
    rhT_hi = tensor("rhT_hi", 52 * K, [2, FC, P], F32R)
    rhT_lo = tensor("rhT_lo", 54 * K, [2, FC, P], F32R)
    yrow = tensor("yrow", 56 * K, [2, D])
    yg = tensor("yg", 64 * K, [GT, TOPK, D])

    top = [205 * K + 512]

    def small(name, dims, dt=F32, parts=P):
        size = 2 if dt == BF16 else 4
        t = tensor(name, top[0], dims, dt, parts)
        top[0] += -(-int(np.prod(dims)) * size // 32) * 32
        return t

    stats = small("stats", [GT, 6])
    mv = small("mv", [GT, 2])
    var_eps = small("var_eps", [GT])
    std = small("std", [GT])
    rstd = small("rstd", [GT])
    nmr = small("nmr", [GT])
    gam_c = small("gam_c", [C])
    bet_c = small("bet_c", [C])
    rwT = small("rwT", [C, E])
    rb_bc = small("rb_bc", [E])
    ramp = small("ramp", [ROUTED + 1])
    before = small("before", [P], BF16)
    ones = small("ones", [P], BF16)
    both = small("both", [NT, E], BF16)
    wts = small("wts", [TOPK, NT])
    pos = small("pos", [TOPK, NT], U32)
    rowv = small("rowv", [NT])
    cnt = small("cnt", [E])
    tiles_e = small("tiles_e", [E])
    ends = small("ends", [E])
    es = ExitStack()
    with es:
        PS = es.enter_context(nc.psum_tensor("PS", [P, 8, D], F32))

        def sem(name):
            return es.enter_context(nc.semaphore(name))

        early_in, late_in = sem("early_in"), sem("late_in")
        x_in = [sem(f"x_in{b}") for b in range(GT)]
        c_in = [sem(f"c_in{b}") for b in range(GT)]
        again_in = [sem(f"again_in{g}") for g in range(NG)]
        zero_ready, zero_done = sem("zero_ready"), sem("zero_done")
        piece_in = [sem("piece_in0"), sem("piece_in1")]
        expert_in = [sem("expert_in0"), sem("expert_in1")]
        expert_taken = sem("expert_taken")
        pieces = sem("pieces")
        pool_chain = sem("pool_chain")
        whT_full, whT_ready, gram_full, gram_hi_ready, gram_ready = (
            sem(n) for n in ("whT_full", "whT_ready", "gram_full", "gram_hi_ready", "gram_ready"))
        rwT_full, rwT_ready = sem("rwT_full"), sem("rwT_ready")
        var1, std1, xh_ready = sem("var1"), sem("std1"), sem("xh_ready")
        px_full, hi_ready, x_split = sem("px_full"), sem("hi_ready"), sem("x_split")
        pc_full, ctxT_ready = sem("pc_full"), sem("ctxT_ready")
        q_full, q_ready = sem("q_full"), sem("q_ready")
        vw_full, vw_done = sem("vw_full"), sem("vw_done")
        s_full, s_taken, at_ready = sem("s_full"), sem("s_taken"), sem("at_ready")
        o_full, var2, std2, nmr_ready, yn_ready = (
            sem(n) for n in ("o_full", "var2", "std2", "nmr_ready", "yn_ready"))
        py_full, py_done = sem("py_full"), sem("py_done")
        m_ready, mhi_ready, m_split = sem("m_ready"), sem("mhi_ready"), sem("m_split")
        z_full, z_taken = sem("z_full"), sem("z_taken")
        var3, std3, xn_ready = sem("var3"), sem("std3"), sem("xn_ready")
        xn_stored = [sem(f"xn_stored{b}") for b in range(GT)]
        max_sub, exp_ready, both_ready, rank_full, pos_ready, tab_ready = (
            sem(n) for n in ("max_sub", "exp_ready", "both_ready", "rank_full", "pos_ready", "tab_ready"))
        stage_in = [sem(f"stage_in{b}") for b in range(GT)]
        scattered = [sem(f"scattered{b}") for b in range(GT)]
        sxhi_ready, sx_split = sem("sxhi_ready"), sem("sx_split")
        sh_full, ssilu_ready, sprod_ready, shhi_ready, sh_split = (
            sem(n) for n in ("sh_full", "ssilu_ready", "sprod_ready", "shhi_ready", "sh_split"))
        sz_full, sz_taken = sem("sz_full"), sem("sz_taken")
        xs_in = [sem(f"xs_in{b}") for b in range(4)]
        rx_full, rxhi_ready, rx_split = sem("rx_full"), sem("rxhi_ready"), sem("rx_split")
        ug_full, rsilu_ready, rprod_ready = sem("ug_full"), sem("rsilu_ready"), sem("rprod_ready")
        rh_full, rhhi_ready, rh_split = sem("rh_full"), sem("rhhi_ready"), sem("rh_split")
        ry_full, ry_ready = sem("ry_full"), sem("ry_ready")
        y_stored = [sem("y_stored0"), sem("y_stored1")]
        yg_in = [sem(f"yg_in{b}") for b in range(GT)]
        yg_taken, out_ready, out_done = sem("yg_taken"), sem("out_ready"), sem("out_done")
        dve_chain = sem("dve_chain")
        dve_passed, pe_passed, pool_passed = sem("dve_passed"), sem("pe_passed"), sem("pool_passed")

        block = es.enter_context(nc.Block())

        def three(ps, w_hi, w_lo, m_hi, m_lo, start, stop):
            nc.tensor.matmul(ps, w_hi, m_hi, start=start, stop=False)
            nc.tensor.matmul(ps, w_hi, m_lo, start=False, stop=False)
            return nc.tensor.matmul(ps, w_lo, m_hi, start=False, stop=stop)


        @block.sync
        def _(sp):
            x_v = x.rearrange("b p d -> p b d")
            sp.dma_start(ident[:], ident_c).then_inc(early_in, 16)
            sp.dma_start(xin[:, 0, :], x[0]).then_inc(x_in[0], 16)
            sp.dma_start(wh_sb[:], wh.rearrange("h d e -> d h e")).then_inc(early_in, 16)
            for b in range(1, GT):
                sp.dma_start(xin[:, b, :], x[b]).then_inc(x_in[b], 16)
            for b in range(GT):
                sp.dma_start(cin[:, b, :], ctx[b]).then_inc(c_in[b], 16)
            sp.dma_start(decay[:], decay_c).then_inc(late_in, 16)
            sp.dma_start(before_f[:], before_c).then_inc(late_in, 16)
            sp.dma_start(ramp[:], ramp_c).then_inc(late_in, 16)
            with nc.allow_non_contiguous_dma("columns of two vectors"):
                sp.dma_start(gam_c[:], gamma.rearrange("(c p) -> p c", p=P)).then_inc(late_in, 16)
                sp.dma_start(bet_c[:], beta.rearrange("(c p) -> p c", p=P)).then_inc(late_in, 16)
            sp.dma_start(lgT[:], rw).then_inc(late_in, 16)
            sp.dma_start(rb_bc[:], rb.unsqueeze(0).broadcast_to([P, E])).then_inc(late_in, 16)
            zt = (ROUTED + 1) // (3 * NG)
            xs_zero = xs_dram.rearrange("(n t p) d -> n p t d", p=P, t=zt)
            sp.wait_ge(zero_ready, 1)

            def zero_fill(g):
                for k in range(3):
                    dst = xs_zero[3 * g + k] if isinstance(g, int) else xs_zero[bass.ds(3 * g + k, 1)].squeeze(0)
                    sp.dma_start(dst, zeros[:].unsqueeze(1).broadcast_to([P, zt, D])).then_inc(zero_done, 16)

            zero_fill(0)
            with sp.Fori(1, NG) as g:
                for b in range(GT):
                    sp.wait_ge(px_full, GT * g + (b - GT + 1))
                    sp.dma_start(xin[:, b, :], x[bass.ds(GT * g + b, 1)].squeeze(0)).then_inc(x_in[b], 16)
                for b in range(GT):
                    sp.wait_ge(pc_full, GT * g + (b - GT + 1))
                    sp.dma_start(cin[:, b, :], ctx[bass.ds(GT * g + b, 1)].squeeze(0)).then_inc(c_in[b], 16)
                zero_fill(g)
            sp.wait_ge(vw_full, 2 * GT * NG)
            for g in range(NG):
                sp.dma_start(x1[:, GT * g:GT * g + GT, :], x_v[:, GT * g:GT * g + GT, :]).then_inc(again_in[g], 16)
            with sp.Fori(0, NG) as g:
                for b in range(GT):
                    sp.wait_ge(xn_ready, GT * g + (b + 1))
                    sp.dma_start(xn_dram[bass.ds(GT * g + b, 1)].squeeze(0), xn[:, b, :]).then_inc(xn_stored[b], 16)
            def expert_pieces(e, k0):
                at = (lambda w: w[e]) if isinstance(e, int) else (lambda w: w[bass.ds(e, 1)].squeeze(0))
                srcs = (at(Wu).rearrange("(c p) f -> p c f", p=P), at(Wg).rearrange("(c p) f -> p c f", p=P),
                        at(Wd).rearrange("(c p) f -> p c f", p=P))
                for k, src in enumerate(srcs):
                    slot = (k0 + k) % 2
                    if isinstance(e, int) and 3 * e + k < 2:
                        sp.wait_ge(pieces, 10)
                    else:
                        sp.wait_ge(expert_taken, 3 * e + (k - 1))
                    dst = raw[:, slot, :].rearrange("p (c f) -> p c f", c=src.shape[1])
                    sp.dma_start(dst, src).then_inc(expert_in[slot], 16)

            for e in range(2):
                expert_pieces(e, 3 * e)
            for b in range(GT):
                sp.wait_ge(xn_stored[b], 16 * NG)
            for b in range(GT):
                sp.wait_ge(max_sub, 1)
                sp.dma_start(stage[:, b, :], xn_dram[b]).then_inc(stage_in[b], 16)
            with sp.Fori(1, NG) as g:
                for b in range(GT):
                    sp.wait_ge(scattered[b], 32 * g)
                    sp.dma_start(stage[:, b, :], xn_dram[bass.ds(GT * g + b, 1)].squeeze(0)).then_inc(stage_in[b], 16)
            with sp.Fori(1, E // 2) as e2:
                for h in range(2):
                    expert_pieces(2 * e2 + h, 3 * h)
            with sp.Fori(0, NT) as j:
                sp.wait_ge(out_ready, j + 1)
                sp.dma_start(out[bass.ds(j, 1)].squeeze(0), x1[:, bass.ds(j, 1), :].squeeze(1)).then_inc(out_done, 16)
            sp.wait_ge(out_done, 16 * NT)

        @block.gpsimd
        def _(pool):
            done = [0]

            def split(src, hi, lo):
                nc.gpsimd.tensor_scalar(hi, src, 1.0, 0.0, ALU.mult, ALU.add).then_inc(pool_chain, 1)
                done[0] += 1
                pool.wait_ge(pool_chain, done[0])
                return nc.gpsimd.tensor_tensor(lo, src, hi.bitcast(F32), ALU.subtract)

            static = []
            for w, hi, lo, free in ((wg, wg_hi, wg_lo, None), (wo, wo_hi, wo_lo, None), (Su[0], su_hi, su_lo, None),
                                    (Sg[0], sg_hi, sg_lo, "scores"), (Sd[0], sd_hi, sd_lo, None)):
                for half in range(2):
                    c = 2 * half
                    static.append((w.rearrange("(c p) f -> p c f", p=P)[:, c:c + 2, :], hi[:, c:c + 2, :], lo[:, c:c + 2, :], free))

            def load_static(k):
                pool.dma_start(raw[:, k % 2, :].rearrange("p (c f) -> p c f", c=2), static[k][0]).then_inc(piece_in[k % 2], 16)

            load_static(0)
            load_static(1)
            for k, (_, hi, lo, free) in enumerate(static):
                if k == 6:
                    pool.wait_ge(at_ready, 1)
                    pool.wait_ge(vw_full, 2 * GT * NG)
                pool.wait_ge(piece_in[k % 2], 16 * (k // 2 + 1))
                split(raw[:, k % 2, :].rearrange("p (c f) -> p c f", c=2), hi, lo).then_inc(pieces, 1)
                if k + 2 < len(static):
                    pool.wait_ge(pieces, k + 1)
                    load_static(k + 2)
            n_static = len(static)
            pool.wait_ge(pieces, n_static)

            def expert_piece(slot, k, par, nth):
                pool.wait_ge(expert_in[par], 16 * nth)
                return split(raw[:, par, :], ring_hi[:, slot, k, :], ring_hi[:, slot, 3 + k, :]).then_inc(expert_taken, 1)

            pool.wait_ge(z_full, GT * NG)
            for e in range(2):
                for k in range(3):
                    n = 3 * e + k
                    expert_piece(e % NSLOT, k, n % 2, n // 2 + 1)
            pool.wait_ge(pos_ready, 1)
            pool.wait_ge(zero_done, 16 * 3 * NG)
            for j in range(NT):
                pool.wait_ge(stage_in[j % GT], 16 * (j // GT + 1))
                for k in range(TOPK):
                    nc.gpsimd.indirect_dma_start(xs_dram, bass.IndirectOffsetOnAxis(ap=pos[:, k, j:j + 1], axis=0),
                                                 stage[:, j % GT, :], None).then_inc(scattered[j % GT], 16)
            pool.wait_ge(sz_full, NT)
            for e in range(2, NSLOT):
                for k in range(3):
                    n = 3 * e + k
                    expert_piece(e % NSLOT, k, n % 2, n // 2 + 1)
            pool.wait_ge(tab_ready, 1)
            base = done[0]
            per = 3 * NSLOT
            with pool.Fori(1, E // NSLOT) as r:
                for s in range(NSLOT):
                    last = pool.value_load(ends_i[0:1, bass.ds(NSLOT * r + (s - NSLOT), 1)], min_val=0, max_val=ROUTED)
                    pool.wait_ge(ry_full, last + 1)
                    for k in range(3):
                        n = 3 * s + k
                        pool.wait_ge(expert_in[n % 2], 16 * (per // 2) * r + 16 * (n // 2 + 1))
                        pool.sem_inc(pool_passed, 1)
                        src = raw[:, n % 2, :]
                        hi, lo = ring_hi[:, s, k, :], ring_hi[:, s, 3 + k, :]
                        nc.gpsimd.tensor_scalar(hi, src, 1.0, 0.0, ALU.mult, ALU.add).then_inc(pool_chain, 1)
                        pool.wait_ge(pool_chain, per * r + (n + 1 + base - per))
                        nc.gpsimd.tensor_tensor(lo, src, hi.bitcast(F32), ALU.subtract).then_inc(expert_taken, 1)
            pool.wait_ge(ry_full, ROUTED + 1)
            pool.wait_ge(expert_taken, 3 * E)
            for par in range(2):
                pool.wait_ge(y_stored[par], 16 * ((ROUTED + 1 - par) // 2))
            for j in range(NT):
                if j >= GT:
                    pool.wait_ge(yg_taken, TOPK * (j - GT + 1))
                for k in range(TOPK):
                    nc.gpsimd.indirect_dma_start(yg[:, j % GT, k, :], None, ys_dram,
                                                 bass.IndirectOffsetOnAxis(ap=pos[:, k, j:j + 1], axis=0)).then_inc(yg_in[j % GT], 16)

        @block.scalar
        def _(act):
            for s in (ctxT_ready, vw_done, py_done):
                act.sem_inc(s, 2)
            act.wait_ge(whT_full, 1)
            nc.scalar.copy(whT[:], PS[:, 0, :].rearrange("p (h d) -> p h d", h=C)).then_inc(whT_ready, 1)
            act.wait_ge(gram_full, 1)
            nc.scalar.copy(gram_hi[:], PS[:, 1, :].rearrange("p (h d) -> p h d", h=C)).then_inc(gram_hi_ready, 1)
            act.wait_ge(rwT_full, 1)
            nc.scalar.copy(rwT[:], PS[:, 4, 0:C * E].rearrange("p (c e) -> p c e", c=C)).then_inc(rwT_ready, 1)
            with act.Fori(0, NG) as g:
                act.wait_ge(var1, g + 1)
                nc.scalar.activation(std[:], var_eps[:], ACT.Sqrt).then_inc(std1, 1)
                for b in range(GT):
                    act.wait_ge(px_full, GT * g + (b + 1))
                    nc.scalar.copy(xhT_hi[:, :, b * P:(b + 1) * P],
                                   PS[:, b % 2, :].rearrange("p (c t) -> p c t", c=C)).then_inc(hi_ready, 1)
                for b in range(GT):
                    act.wait_ge(pc_full, GT * g + (b + 1))
                    nc.scalar.copy(ctxT[:, b], PS[:, 2 + b % 2, :].rearrange("p (c t) -> p c t", c=C)).then_inc(ctxT_ready, 1)
                for b in range(GT):
                    act.wait_ge(vw_full, 2 * GT * g + (b + 1))
                    nc.scalar.copy(vals[:, :, bass.ds(GT * g + b, 1), :].squeeze(2),
                                   PS[:, 5 + b % 2, :].rearrange("p (h d) -> p h d", h=C)).then_inc(vw_done, 1)
                for c in range(C):
                    act.wait_ge(vw_full, 2 * GT * g + (GT + c + 1))
                    nc.scalar.activation(gate[:, bass.ds(g, 1), c, :].squeeze(1), PS[:, 5 + c % 2, :], ACT.Relu).then_inc(vw_done, 1)

            def x2_copy(g, o):
                for b in range(GT):
                    act.wait_ge(py_full, o + b + 1)
                    dst = x2T[:, g, :, b * P:(b + 1) * P] if isinstance(g, int) else x2T[:, bass.ds(g, 1), :, b * P:(b + 1) * P].squeeze(1)
                    nc.scalar.copy(dst, PS[:, 4 + b % 2, :].rearrange("p (c t) -> p c t", c=C)).then_inc(py_done, 1)

            def lgT_copy(o):
                act.wait_ge(py_full, o + 1)
                nc.scalar.copy(lgT[:], PS[0:E, 4, :]).then_inc(py_done, 1)

            def lg_copy(g, o):
                act.wait_ge(py_full, o + 1)
                dst = logits[:, GT * g:GT * g + GT, :] if isinstance(g, int) else logits[:, bass.ds(GT * g, GT), :]
                nc.scalar.copy(dst, PS[:, 5, 0:GT * E].rearrange("p (b e) -> p b e", b=GT)).then_inc(py_done, 1)

            def attend(g, first):
                o = 0 if first else 10 * g - 6
                act.wait_ge(var2, g + 1)
                nc.scalar.activation(std[:], var_eps[:], ACT.Sqrt).then_inc(std2, 1)
                act.wait_ge(nmr_ready, g + 1)
                for b in range(GT):
                    nc.scalar.activation(yn[:, b, :].rearrange("p (h d) -> p h d", h=C), PS[:, 0:4, b * P:(b + 1) * P],
                                         ACT.Identity, bias=nmr[:, b:b + 1], scale=rstd[:, b:b + 1]).then_inc(yn_ready, 1)
                if not first:
                    x2_copy(g - 1, o)
                    o = o + 4
                else:
                    act.wait_ge(late_in, 16 * 7)
                for c in range(C):
                    act.wait_ge(py_full, o + c + 1)
                    nc.scalar.activation(ya[:, c, :], PS[:, 4 + c % 2, :], ACT.Identity,
                                         bias=bet_c[:, c:c + 1], scale=gam_c[:, c:c + 1]).then_inc(py_done, 1)
                for c in range(C):
                    act.wait_ge(m_ready, C * g + (c + 1))
                    src = gate[:, g, c, :] if first else gate[:, bass.ds(g, 1), c, :].squeeze(1)
                    nc.scalar.copy(mT_hi[:, c, :], src).then_inc(mhi_ready, 1)
                if not first:
                    lgT_copy(o + 4)
                    lg_copy(g - 1, o + 5)
                act.wait_ge(var3, g + 1)
                nc.scalar.activation(std[:], var_eps[:], ACT.Sqrt).then_inc(std3, 1)

            act.wait_ge(zero_done, 16 * 3 * NG)
            attend(0, True)
            with act.Fori(1, NG) as g:
                attend(g, False)
            o = 10 * NG - 6
            x2_copy(NG - 1, o)
            lgT_copy(o + 4)
            lg_copy(NG - 1, o + 5)

            def shared_half(k, g, h):
                src = x2T[:, bass.ds(g, 1), :, h * HW:(h + 1) * HW].squeeze(1)
                act.wait_ge(sh_full, C * k + 1)
                nc.scalar.copy(sx_hi[:], src).then_inc(sxhi_ready, 1)

                def hi(f):
                    act.wait_ge(sprod_ready, C * k + (f + 3))
                    nc.scalar.copy(shT_hi[:, f, :], s_prod[:, f % 2, :]).then_inc(shhi_ready, 1)

                for f in range(C):
                    act.wait_ge(sh_full, C * k + (f + 2))
                    nc.scalar.activation(s_silu[:, f % 2, :], PS[:, f % 2, 0:HW], ACT.Silu).then_inc(ssilu_ready, 1)
                    if f:
                        hi(f - 1)
                hi(C - 1)

            act.wait_ge(max_sub, 1)
            nc.scalar.activation(expl[:], tmp[:], ACT.Exp).then_inc(exp_ready, 1)
            act.wait_ge(m_split, C * NG)
            act.wait_ge(z_full, GT * NG)
            act.wait_ge(py_done, 2 + 10 * NG)
            with act.Fori(0, NG) as g:
                for h in range(2):
                    shared_half(2 * g + h, g, h)

            def load_xs(t, b):
                act.dma_start(xs[:, b, :], xs_dram[bass.ds(t * P, P), :] if not isinstance(t, int) else xs_dram[t * P:(t + 1) * P, :]
                              ).then_inc(xs_in[b], 16)

            def x_hi(n, par):
                act.wait_ge(rx_full, n + 1)
                nc.scalar.copy(xsT_hi[:, par], PS[:, par, :].rearrange("p (c t) -> p c t", c=C)).then_inc(rxhi_ready, 1)

            def silu(n, par):
                act.wait_ge(ug_full, n + 1)
                nc.scalar.activation(r_silu[:, par, :], PS[:, 2 + par, 0:FE], ACT.Silu).then_inc(rsilu_ready, 1)

            def h_hi(n, par):
                act.wait_ge(rh_full, n + 1)
                nc.scalar.copy(rhT_hi[:, par], PS[:, 4, 0:FE].rearrange("p (c t) -> p c t", c=FC)).then_inc(rhhi_ready, 1)

            def y_out(n, par, stored):
                if not isinstance(stored, int) or stored > 0:
                    act.wait_ge(y_stored[par], stored)
                act.wait_ge(ry_full, n + 2)
                nc.scalar.copy(yrow[:, par, :], PS[:, 6 + par, :]).then_inc(ry_ready, 1)
                act.wait_ge(ry_ready, n + 1)
                dst = ys_dram[n * P:(n + 1) * P, :] if isinstance(n, int) else ys_dram[bass.ds(n * P, P), :]
                act.dma_start(dst, yrow[:, par, :]).then_inc(y_stored[par], 16)

            for b in range(GT):
                act.wait_ge(scattered[b], 32 * NG)
            act.wait_ge(sz_full, NT)
            for t in range(4):
                load_xs(t, t)
            x_hi(0, 0)
            x_hi(1, 1)
            silu(0, 0)

            def step(i, k, stored):
                par = k % 2
                if stored is not None:
                    y_out(i - 1, 1 - par, stored)
                x_hi(i + 2, par)
                if not isinstance(i, int) or i + 4 <= ROUTED:
                    load_xs(i + 4, k)
                h_hi(i, par)
                silu(i + 1, 1 - par)

            for i in range(4):
                step(i, i, None if i == 0 else 16 * ((i - 1) // 2))
            last = (ROUTED - 3) // 4
            with act.Fori(1, last) as q:
                for k in range(4):
                    step(4 * q + k, k, 32 * q + 16 * ((k - 1) // 2))
            for i in range(4 * last, ROUTED - 1):
                step(i, i % 4, 16 * ((i - 1) // 2))
            i = ROUTED - 1
            y_out(i - 1, (i - 1) % 2, 16 * ((i - 1) // 2))
            h_hi(i, i % 2)
            y_out(i, i % 2, 16 * (i // 2))

        @block.vector
        def _(dve):
            ticks = [0]

            def pass_on():
                dve.sem_inc(dve_passed, 1)

            def link(ins, plain=False):
                ticks[0] = ticks[0] + 1
                ins.then_inc(dve_chain, 1)
                dve.wait_ge(dve_chain, ticks[0])
                if plain:
                    pass_on()

            for s in (x_split, z_taken, sprod_ready, sh_split, rx_split, sz_taken):
                dve.sem_inc(s, 2)
            for s in (q_ready, s_taken, rh_split):
                dve.sem_inc(s, 1)
            nc.vector.memset(zeros[:], 0.0).then_inc(zero_ready, 1)
            nc.vector.memset(ones[:], 1.0)
            link(nc.vector.memset(scores[:], 0.0))
            dve.wait_ge(gram_hi_ready, 1)
            nc.vector.tensor_tensor(gram_lo[:], PS[:, 1, :].rearrange("p (h d) -> p h d", h=C),
                                    gram_hi[:].bitcast(F32), ALU.subtract).then_inc(gram_ready, 1)

            def normal(srcs, eps, var_sem, std_sem, n, n_std):
                for b, src in enumerate(srcs):
                    i = nc.vector.bn_stats(stats[:, b, :], src)
                link(i, plain=True)
                for b in range(GT):
                    i = nc.vector.bn_aggr(mv[:, b, :], stats[:, b, :])
                link(i)
                nc.vector.tensor_scalar(var_eps[:], mv[:, :, 1], eps, None, ALU.add).then_inc(var_sem, 1)
                dve.wait_ge(std_sem, n_std)
                return nc.vector.reciprocal(rstd[:], std[:])

            base = ticks[0]
            per = 4
            with dve.Fori(0, NG) as g:
                ticks[0] = per * g + base
                for b in range(GT):
                    dve.wait_ge(x_in[b], 16 * g + 16)
                link(normal([xin[:, b, :] for b in range(GT)], LN_EPS, var1, std1, g, g + 1))
                for b in range(GT):
                    nc.vector.tensor_scalar(xin[:, b, :], xin[:, b, :], mv[:, b, 0:1], rstd[:, b:b + 1],
                                            ALU.subtract, ALU.mult).then_inc(xh_ready, 1)
                for b in range(GT):
                    dve.wait_ge(hi_ready, GT * g + (b + 1))
                    nc.vector.tensor_tensor(xhT_lo[:, :, b * P:(b + 1) * P], PS[:, b % 2, :].rearrange("p (c t) -> p c t", c=C),
                                            xhT_hi[:, :, b * P:(b + 1) * P].bitcast(F32), ALU.subtract).then_inc(x_split, 1)
                for h in range(C):
                    dve.wait_ge(q_full, C * g + (h + 1))
                    nc.vector.tensor_copy(qT[:, h, :], PS[:, 4, :]).then_inc(q_ready, 1)
                dve.wait_ge(s_full, g + 1)
                ins = nc.vector.tensor_tensor(scores[:], PS[:, 7, :].rearrange("p (h s) -> p h s", h=C), scores[:], ALU.add)
                ins.then_inc(s_taken, 1)
                dve.wait_ge(s_taken, g + 2)
                link(nc.vector.tensor_copy(rowv[:, 0:1], scores[:, 0, 0:1]))
            ticks[0] = base + per * NG
            dve.wait_ge(late_in, 16 * 7)
            nc.vector.tensor_copy(before[:], before_f[:])
            link(nc.vector.tensor_tensor(scores[:], scores[:], decay[:], ALU.mult))
            link(nc.vector.scalar_tensor_tensor(scores[:], scores[:], -1.0, scores[:], ALU.mult, ALU.max))
            nc.vector.tensor_scalar(scores[:], scores[:], 1.0, None, ALU.max).then_inc(at_ready, 1)

            def attend(g, first):
                dve.wait_ge(o_full, g + 1)
                link(normal([PS[:, 0:4, b * P:(b + 1) * P] for b in range(GT)], GN_EPS, var2, std2, g, g + 1))
                nc.vector.scalar_tensor_tensor(nmr[:], mv[:, :, 0], -1.0, rstd[:], ALU.mult, ALU.mult).then_inc(nmr_ready, 1)
                gt = [gate[:, g, c, :] if first else gate[:, bass.ds(g, 1), c, :].squeeze(1) for c in range(C)]
                o = 2 + (0 if first else 10 * g - 2)
                for c in range(C):
                    dve.wait_ge(py_done, o + (c + 1))
                    nc.vector.tensor_tensor(gt[c], ya[:, c, :], gt[c], ALU.mult).then_inc(m_ready, 1)
                for c in range(C):
                    dve.wait_ge(mhi_ready, C * g + (c + 1))
                    nc.vector.tensor_tensor(mT_lo[:, c, :], gt[c], mT_hi[:, c, :].bitcast(F32), ALU.subtract).then_inc(m_split, 1)
                if first:
                    for k in range(NG):
                        dve.wait_ge(again_in[k], 16)
                rows = [x1[:, b, :] if first else x1[:, bass.ds(GT * g + b, 1), :].squeeze(1) for b in range(GT)]
                for b in range(GT):
                    dve.wait_ge(z_full, GT * g + (b + 1))
                    nc.vector.tensor_tensor(rows[b], PS[:, 6 + b % 2, :], rows[b], ALU.add).then_inc(z_taken, 1)
                dve.wait_ge(z_taken, GT * g + (GT + 2))
                pass_on()
                link(normal(rows, LN_EPS, var3, std3, g, g + 1))
                for b in range(GT):
                    if not first:
                        dve.wait_ge(xn_stored[b], 16 * g)
                        dve.wait_ge(py_full, 10 * g - 6 + (b + 1))
                    nc.vector.tensor_scalar(xn[:, b, :], rows[b], mv[:, b, 0:1], rstd[:, b:b + 1],
                                            ALU.subtract, ALU.mult).then_inc(xn_ready, 1)

            dve.wait_ge(zero_done, 16 * 3 * NG)
            attend(0, True)
            base = ticks[0]
            per = 6
            with dve.Fori(1, NG) as g:
                ticks[0] = per * g + (base - per)
                attend(g, False)
            ticks[0] = base + per * (NG - 1)

            def bc_t(v):
                return v.unsqueeze(1).broadcast_to([P, NT, E])

            def bc_e(v):
                return v.unsqueeze(2).broadcast_to([P, NT, E])

            dve.wait_ge(py_done, 2 + 10 * NG)
            nc.vector.tensor_reduce(rowv[:], logits[:], AX.X, ALU.max)
            link(nc.vector.tensor_tensor(rank[:], logits[:], bc_t(rb_bc[:]), ALU.add))
            nc.vector.tensor_tensor(tmp[:], logits[:], bc_e(rowv[:]), ALU.subtract).then_inc(max_sub, 1)
            for j in range(NT):
                ins = nc.vector.max(top8[:, j, :], rank[:, j, :])
            link(ins)
            for j in range(NT):
                ins = nc.vector.max_index(top8i[:, j, :], top8[:, j, :], rank[:, j, :])
            link(ins)
            for k in range(TOPK):
                link(nc.vector.tensor_copy(rowv[:], top8i[:, :, k]))
                link(nc.vector.tensor_tensor(oh[:, k], bc_t(ramp[:, 0:E]), bc_e(rowv[:]), ALU.is_equal))
            nc.vector.tensor_tensor(both[:], oh[:, 0], oh[:, 1], ALU.add).then_inc(both_ready, 1)
            dve.wait_ge(exp_ready, 1)
            for k in range(TOPK):
                link(nc.vector.tensor_tensor(tmp[:], oh[:, k], expl[:], ALU.mult))
                link(nc.vector.tensor_reduce(wts[:, k, :], tmp[:], AX.X, ALU.add))
            link(nc.vector.tensor_tensor(rowv[:], wts[:, 0, :], wts[:, 1, :], ALU.add))
            link(nc.vector.reciprocal(rowv[:], rowv[:]))
            for k in range(TOPK):
                nc.vector.tensor_tensor(wts[:, k, :], wts[:, k, :], rowv[:], ALU.mult)
            dve.wait_ge(rank_full, 1)
            link(nc.vector.tensor_scalar(cnt[:], PS[:, 4, NT * E:NT * E + E], 1.0, None, ALU.max))
            link(nc.vector.tensor_scalar(tmp[:], bc_e(ramp[:, 0:NT]), float(P), None, ALU.mult))
            link(nc.vector.tensor_tensor(tmp[:], bc_t(cnt[:]), tmp[:], ALU.is_gt))
            link(nc.vector.tensor_reduce(tiles_e[:], tmp[:].rearrange("p k e -> p e k"), AX.X, ALU.add))
            link(nc.vector.tensor_tensor_scan(ends[:], tiles_e[:], tiles_e[:], 0.0, ALU.add, ALU.bypass))
            link(nc.vector.tensor_tensor(tiles_e[:], ends[:], tiles_e[:], ALU.subtract))
            link(nc.vector.tensor_scalar(tiles_e[:], tiles_e[:], float(P), None, ALU.mult))
            link(nc.vector.tensor_tensor(rank[:], PS[:, 4, 0:NT * E].rearrange("p (t e) -> p t e", t=NT), bc_t(tiles_e[:]), ALU.add))
            for k in range(TOPK):
                link(nc.vector.tensor_tensor(tmp[:], oh[:, k], rank[:], ALU.mult))
                link(nc.vector.tensor_reduce(rowv[:], tmp[:], AX.X, ALU.add))
                ins = nc.vector.tensor_copy(pos[:, k, :], rowv[:])
                if k < TOPK - 1:
                    link(ins)
            ins.then_inc(pos_ready, 1)
            nc.vector.tensor_copy(ends_i[:], ends[0:1, :])
            link(nc.vector.tensor_tensor(tcmp[:], ends[0:1, :].unsqueeze(1).broadcast_to([1, ROUTED, E]),
                                         ramp[0:1, 0:ROUTED].unsqueeze(2).broadcast_to([1, ROUTED, E]), ALU.is_le))
            link(nc.vector.tensor_reduce(tab_f[:], tcmp[:], AX.X, ALU.add))
            link(nc.vector.tensor_scalar(tab_f[:], tab_f[:], float(E - 1), None, ALU.min))
            link(nc.vector.tensor_copy(tab_e[:], tab_f[:]))
            nc.vector.tensor_scalar(tab_s[:], tab_e[:], NSLOT - 1, None, ALU.bitwise_and).then_inc(tab_ready, 1)

            def shared_half(k, g, h):
                src = x2T[:, bass.ds(g, 1), :, h * HW:(h + 1) * HW].squeeze(1)
                dve.wait_ge(sxhi_ready, k + 1)
                nc.vector.tensor_tensor(sx_lo[:], src, sx_hi[:].bitcast(F32), ALU.subtract).then_inc(sx_split, 1)

                def lo(f):
                    dve.wait_ge(shhi_ready, C * k + (f + 1))
                    nc.vector.tensor_tensor(shT_lo[:, f, :], s_prod[:, f % 2, :], shT_hi[:, f, :].bitcast(F32),
                                            ALU.subtract).then_inc(sh_split, 1)

                for f in range(C):
                    dve.wait_ge(ssilu_ready, C * k + (f + 1))
                    dve.wait_ge(sh_split, C * k + (f + 1))
                    nc.vector.tensor_tensor(s_prod[:, f % 2, :], PS[:, f % 2, HW:2 * HW], s_silu[:, f % 2, :], ALU.mult).then_inc(sprod_ready, 1)
                    if f:
                        lo(f - 1)
                lo(C - 1)
                for b in range(2):
                    dve.wait_ge(sz_full, 2 * k + (b + 1))
                    row = x1[:, bass.ds(GT * g + (2 * h + b), 1), :].squeeze(1)
                    nc.vector.tensor_tensor(row, PS[:, 2 + b, :], row, ALU.add).then_inc(sz_taken, 1)

            with dve.Fori(0, NG) as g:
                for h in range(2):
                    shared_half(2 * g + h, g, h)

            def x_lo(n, par):
                dve.wait_ge(rxhi_ready, n + 1)
                nc.vector.tensor_tensor(xsT_lo[:, par], PS[:, par, :].rearrange("p (c t) -> p c t", c=C),
                                        xsT_hi[:, par].bitcast(F32), ALU.subtract).then_inc(rx_split, 1)

            def prod(n, par):
                dve.wait_ge(rsilu_ready, n + 1)
                nc.vector.tensor_tensor(r_prod[:, par, :], PS[:, 2 + par, FE:2 * FE], r_silu[:, par, :], ALU.mult).then_inc(rprod_ready, 1)

            def h_lo(n, par):
                dve.wait_ge(rhhi_ready, n + 1)
                nc.vector.tensor_tensor(rhT_lo[:, par], PS[:, 4, 0:FE].rearrange("p (c t) -> p c t", c=FC),
                                        rhT_hi[:, par].bitcast(F32), ALU.subtract).then_inc(rh_split, 1)

            x_lo(0, 0)
            x_lo(1, 1)
            prod(0, 0)
            with dve.Fori(0, (ROUTED - 1) // 2) as q:
                for par in range(2):
                    i = 2 * q + par
                    x_lo(i + 2, par)
                    h_lo(i, par)
                    prod(i + 1, 1 - par)
            h_lo(ROUTED - 1, (ROUTED - 1) % 2)

            dve.wait_ge(sz_taken, NT + 2)
            with dve.Fori(0, NG) as g:
                for b in range(GT):
                    dve.wait_ge(yg_in[b], 32 * g + 32)
                    row = x1[:, bass.ds(GT * g + b, 1), :].squeeze(1)
                    for k in range(TOPK):
                        ins = nc.vector.scalar_tensor_tensor(row, yg[:, b, k, :], wts[:, k, bass.ds(GT * g + b, 1)], row, ALU.mult, ALU.add)
                        if k == 0:
                            ins.then_inc(yg_taken, 1)
                            dve.wait_ge(yg_taken, 2 * GT * g + (2 * b + 1))
                    ins.then_inc(yg_taken, 1)
                    dve.wait_ge(yg_taken, 2 * GT * g + (2 * b + 2))
                    dve.sem_inc(out_ready, 1)

        @block.tensor
        def _(pe):
            def transposes(bank, srcs, width=P):
                for c, s in enumerate(srcs):
                    ins = nc.tensor.transpose(PS[:, bank, c * width:(c + 1) * width], s, ident[0:s.shape[0], 0:s.shape[0]])
                return ins

            for s in (sh_full, ry_full):
                pe.sem_inc(s, 1)
            pe.wait_ge(early_in, 32)
            transposes(0, [wh_sb[:, h, :] for h in range(C)]).then_inc(whT_full, 1)
            pe.wait_ge(whT_ready, 1)
            for h in range(C):
                ins = nc.tensor.matmul(PS[:, 1, h * P:(h + 1) * P], whT[:, h, :], whT[:, h, :], start=True, stop=True)
            ins.then_inc(gram_full, 1)
            pe.wait_ge(late_in, 16 * 7)
            transposes(4, [lgT[:, c * P:(c + 1) * P] for c in range(C)], E).then_inc(rwT_full, 1)
            pe.wait_ge(gram_ready, 1)
            pe.wait_ge(rwT_ready, 1)
            with pe.Fori(0, NG) as g:
                for b in range(GT):
                    pe.wait_ge(xh_ready, GT * g + (b + 1))
                    pe.wait_ge(x_split, GT * g + (b + 1))
                    transposes(b % 2, [xin[:, b, c * P:(c + 1) * P] for c in range(C)]).then_inc(px_full, 1)
                for b in range(GT):
                    pe.wait_ge(c_in[b], 16 * g + 16)
                    pe.wait_ge(ctxT_ready, GT * g + (b + 1))
                    transposes(2 + b % 2, [cin[:, b, c * P:(c + 1) * P] for c in range(C)]).then_inc(pc_full, 1)
                pe.wait_ge(x_split, GT * g + (2 + GT))
                pe.wait_ge(ctxT_ready, GT * g + (2 + GT))

                def q_mm(h):
                    pe.wait_ge(q_ready, C * g + (h + 1))
                    three(PS[:, 4, :], gram_hi[:, h, :], gram_lo[:, h, :], xhT_hi[:, h, :], xhT_lo[:, h, :],
                          True, True).then_inc(q_full, 1)

                def s_mm(h):
                    pe.wait_ge(q_ready, C * g + (h + 2))
                    if h == 0:
                        pe.wait_ge(s_taken, g + 1)
                    for b in range(GT):
                        ins = nc.tensor.matmul(PS[:, 7, h * P:(h + 1) * P], ctxT[:, b, h, :], qT[:, h, b * P:(b + 1) * P],
                                               start=(b == 0), stop=(b == GT - 1))
                    if h == C - 1:
                        ins.then_inc(s_full, 1)

                def v_mm(b):
                    pe.wait_ge(vw_done, 2 * GT * g + (b + 1))
                    for h in range(C):
                        ins = nc.tensor.matmul(PS[:, 5 + b % 2, h * P:(h + 1) * P], ctxT[:, b, h, :], wh_sb[:, h, :],
                                               start=True, stop=True)
                    ins.then_inc(vw_full, 1)

                q_mm(0)
                v_mm(0)
                for h in range(1, C):
                    q_mm(h)
                    s_mm(h - 1)
                    v_mm(h)
                s_mm(C - 1)
                pe.wait_ge(pieces, 2)
                for o in range(C):
                    pe.wait_ge(vw_done, 2 * GT * g + (GT + o + 1))
                    for c in range(C):
                        ins = three(PS[:, 5 + o % 2, :], wg_hi[:, c, o * P:(o + 1) * P], wg_lo[:, c, o * P:(o + 1) * P],
                                    xhT_hi[:, c, :], xhT_lo[:, c, :], c == 0, c == C - 1)
                    ins.then_inc(vw_full, 1)

            def x2_transposes(g, o):
                for b in range(GT):
                    pe.wait_ge(xn_ready, GT * g + (b + 1))
                    pe.wait_ge(py_done, o + (b + 1))
                    transposes(4 + b % 2, [xn[:, b, c * P:(c + 1) * P] for c in range(C)]).then_inc(py_full, 1)

            def logits_mm(g, o):
                pe.wait_ge(py_done, o + 1)
                for c in range(C):
                    src = x2T[:, g, c, :] if isinstance(g, int) else x2T[:, bass.ds(g, 1), c, :].squeeze(1)
                    ins = nc.tensor.matmul(PS[0:E, 4, :], rwT[:, c, :], src, start=(c == 0), stop=(c == C - 1))
                ins.then_inc(py_full, 1)

            def logits_turn(o):
                pe.wait_ge(py_done, o + 2)
                pe.sem_inc(pe_passed, 1)
                transposes(5, [lgT[:, b * P:(b + 1) * P] for b in range(GT)], E).then_inc(py_full, 1)

            def attend(g, first):
                o = 0 if first else 10 * g - 6
                if not first:
                    pe.wait_ge(yn_ready, GT * g)
                for h in range(C):
                    v = vals[:, h, GT * g:GT * g + GT, :] if first else vals[:, h, bass.ds(GT * g, GT), :]
                    ins = nc.tensor.matmul(PS[:, h, :].rearrange("p (b d) -> p b d", b=GT), scores[:, h, :], v, start=True, stop=True)
                ins.then_inc(o_full, 1)
                if not first:
                    x2_transposes(g - 1, o)
                    o = o + 4
                pe.wait_ge(yn_ready, GT * g + GT)
                for c in range(C):
                    pe.wait_ge(py_done, o + (c + 1))
                    transposes(4 + c % 2, [yn[:, b, c * P:(c + 1) * P] for b in range(GT)]).then_inc(py_full, 1)
                if not first:
                    pe.wait_ge(py_done, o + 2)
                    logits_mm(g - 1, o + 4)
                pe.wait_ge(m_split, C * g + C)
                for b in range(GT):
                    pe.wait_ge(z_taken, GT * g + (b + 1))
                    for c in range(C):
                        ins = three(PS[:, 6 + b % 2, :], mT_hi[:, c, b * P:(b + 1) * P], mT_lo[:, c, b * P:(b + 1) * P],
                                    wo_hi[:, c, :], wo_lo[:, c, :], c == 0, c == C - 1)
                    ins.then_inc(z_full, 1)
                if not first:
                    logits_turn(o + 5)

            pe.wait_ge(at_ready, 1)
            pe.wait_ge(vw_done, 2 + 2 * GT * NG)
            pe.wait_ge(pieces, 4)
            attend(0, True)
            with pe.Fori(1, NG) as g:
                attend(g, False)
            o = 10 * NG - 6
            x2_transposes(NG - 1, o)
            pe.wait_ge(py_done, o + 6)
            logits_mm(NG - 1, o + 4)
            logits_turn(o + 5)

            def ranks():
                pe.wait_ge(both_ready, 1)
                R = PS[:, 4, 0:NT * E].rearrange("p (t e) -> p t e", t=NT)
                nc.tensor.matmul(R, before[:], both[:], start=True, stop=False)
                for t in range(NT - 1):
                    nc.tensor.matmul(R[:, t + 1:NT, :], ones[:], both[:, t:t + 1, :].broadcast_to([P, NT - 1 - t, E]),
                                     start=False, stop=(t == NT - 2))
                for t in range(NT):
                    ins = nc.tensor.matmul(PS[:, 4, NT * E:NT * E + E], ones[:], both[:, t, :], start=(t == 0), stop=(t == NT - 1))
                ins.then_inc(rank_full, 1)

            pe.wait_ge(yn_ready, GT * NG)
            pe.wait_ge(pieces, 10)
            ranks()
            with pe.Fori(0, NG) as g:
                for h in range(2):
                    k = 2 * g + h
                    pe.wait_ge(sx_split, k + 1)
                    for f in range(C):
                        pe.wait_ge(sprod_ready, C * k + (f + 1))
                        for part, (w_hi, w_lo) in enumerate(((su_hi, su_lo), (sg_hi, sg_lo))):
                            for c in range(C):
                                ins = three(PS[:, f % 2, part * HW:(part + 1) * HW], w_hi[:, c, f * P:(f + 1) * P],
                                            w_lo[:, c, f * P:(f + 1) * P], sx_hi[:, c, :], sx_lo[:, c, :], c == 0, c == C - 1)
                        ins.then_inc(sh_full, 1)
                    pe.wait_ge(sz_taken, 2 * k + 2)
                    for f in range(C):
                        pe.wait_ge(sh_split, C * k + (f + 3))
                        for b in range(2):
                            ins = three(PS[:, 2 + b, :], shT_hi[:, f, b * P:(b + 1) * P], shT_lo[:, f, b * P:(b + 1) * P],
                                        sd_hi[:, f, :], sd_lo[:, f, :], f == 0, f == C - 1)
                            if f == C - 1:
                                ins.then_inc(sz_full, 1)

            def x_turn(n, par, b, loads):
                pe.wait_ge(xs_in[b], loads)
                pe.wait_ge(rx_split, n + 1)
                transposes(par, [xs[:, b, c * P:(c + 1) * P] for c in range(C)]).then_inc(rx_full, 1)

            def up(n, par, e, slot):
                pe.wait_ge(expert_taken, 3 * e + 2)
                pe.wait_ge(rx_split, n + 3)
                W = ring_hi[:, bass.ds(slot, 1), :, :].squeeze(1)
                ps = PS[:, 2 + par, :].rearrange("p (a f) -> p a f", a=2)
                for c in range(C):
                    hi = W[:, 0:2, c * FE:(c + 1) * FE]
                    lo = W[:, 3:5, c * FE:(c + 1) * FE]
                    ins = three(ps, xsT_hi[:, par, c, :], xsT_lo[:, par, c, :], hi, lo, c == 0, c == C - 1)
                ins.then_inc(ug_full, 1)

            def h_turn(n, par):
                pe.wait_ge(rprod_ready, n + 1)
                pe.wait_ge(rh_split, n + 1)
                transposes(4, [r_prod[:, par, c * P:(c + 1) * P] for c in range(FC)]).then_inc(rh_full, 1)

            def down(n, par, e, slot):
                pe.wait_ge(expert_taken, 3 * e + 3)
                pe.wait_ge(rh_split, n + 2)
                W = ring_hi[:, bass.ds(slot, 1), :, :].squeeze(1)
                for f in range(FC):
                    ins = three(PS[:, 6 + par, :], rhT_hi[:, par, f, :], rhT_lo[:, par, f, :],
                                W[:, 2, f * D:(f + 1) * D], W[:, 5, f * D:(f + 1) * D], f == 0, f == FC - 1)
                ins.then_inc(ry_full, 1)

            def tile_weights(n):
                at = (lambda t: t[0:1, n:n + 1]) if isinstance(n, int) else (lambda t: t[0:1, bass.ds(n, 1)])
                return (pe.value_load(at(tab_e), min_val=0, max_val=E - 1),
                        pe.value_load(at(tab_s), min_val=0, max_val=NSLOT - 1))

            def step(i, par, b, loads):
                x_turn(i + 2, par, b, loads)
                h_turn(i, par)
                e, slot = tile_weights(i + 1)
                up(i + 1, 1 - par, e, slot)
                e, slot = tile_weights(i)
                if not isinstance(i, int) or i >= 2:
                    pe.wait_ge(ry_ready, i - 1)
                down(i, par, e, slot)

            pe.wait_ge(tab_ready, 1)
            pe.wait_ge(sz_taken, NT + 2)
            x_turn(0, 0, 0, 16)
            x_turn(1, 1, 1, 16)
            up(0, 0, *tile_weights(0))
            step(0, 0, 2, 16)
            step(1, 1, 3, 16)
            n_full = (ROUTED - 1 - 2) // 4
            with pe.Fori(0, n_full) as q:
                for k in range(4):
                    step(4 * q + (2 + k), k % 2, k, 16 * q + 32)
            for i in range(2 + 4 * n_full, ROUTED - 1):
                step(i, i % 2, (i + 2) % 4, 16 * ((i + 2) // 4 + 1))
            i = ROUTED - 1
            h_turn(i, i % 2)
            pe.wait_ge(ry_ready, i - 1)
            down(i, i % 2, *tile_weights(i))


_INS = {"x": "x", "ctx_2048": "ctx", "L0_xattn_Wh": "wh", "L0_xattn_wg_w": "wg", "L0_xattn_wo_w": "wo",
        "L0_xattn_gn_gamma": "gamma", "L0_xattn_gn_beta": "beta", "L0_ffn_router_w": "rw",
        "L0_ffn_router_bias": "rb", "L0_ffn_Wu": "Wu", "L0_ffn_Wg": "Wg", "L0_ffn_Wd": "Wd",
        "L0_ffn_Su": "Su", "L0_ffn_Sg": "Sg", "L0_ffn_Sd": "Sd"}


def shape_constants():
    return {
        "ident_c": np.eye(P, dtype=np.float32),
        "decay_c": decay_over_root(C, P, P),
        "before_c": np.triu(np.ones((P, P), np.float32), 1),
        "ramp_c": np.tile(np.arange(ROUTED + 1, dtype=np.float32), (P, 1)),
    }


def kernel(**inputs):
    import concourse.bacc as bacc
    from concourse.bass_utils import run_bass_kernel_spmd

    nc = bacc.Bacc("TRN2", target_bir_lowering=False, num_devices=1)
    arrays, args = {}, {}
    for name, arg in _INS.items():
        arrays[f"in_{arg}"] = np.ascontiguousarray(inputs[name])
    for arg, a in shape_constants().items():
        arrays[f"in_{arg}"] = a
    for name, a in arrays.items():
        args[name[3:]] = nc.dram_tensor(name, a.shape, mybir.dt.from_np(a.dtype), kind="ExternalInput").ap()
    out = nc.dram_tensor("out_rows", (NT, P, D), F32, kind="ExternalOutput").ap()
    xattn_moe(nc, **args, out=out)
    r = run_bass_kernel_spmd(nc, [arrays], core_ids=[0])
    return r.results[0]["out_rows"]
```

```python
import numpy as np
from contextlib import ExitStack

import concourse.bass as bass
from concourse import mybir

F32 = mybir.dt.float32
F32R = mybir.dt.float32r
BF16 = mybir.dt.bfloat16
I32 = mybir.dt.int32
U32 = mybir.dt.uint32
ALU = mybir.AluOpType
ACT = mybir.ActivationFunctionType
AX = mybir.AxisListType

P = 128
D = 512
C = D // P
NT = 16
GT = 4
NG = NT // GT
GW = GT * P
E = 16
FE = 256
FC = FE // P
TOPK = 2
ROUTED = (NT * P * TOPK + E * (P - 1)) // P
NSLOT = 4
PIECE = 1024
LN_EPS = 1e-5
GN_EPS = 1e-3


def decay_over_root(heads, s, hd):
    gam = (1.0 - 2.0 ** (-5.0 - np.arange(heads, dtype=np.float32))).astype(np.float32)
    expo = np.arange(s, dtype=np.float32)[None, :] - np.arange(s, dtype=np.float32)[:, None]
    d = np.where(expo[None] <= 0, gam[:, None, None] ** expo[None], np.float32(0.0)).astype(np.float32)
    d = d / np.sqrt(d.sum(axis=-1))[:, None, :]
    return np.ascontiguousarray(d.transpose(2, 0, 1) / np.float32(np.sqrt(hd))).astype(np.float32)


def xattn_moe(nc, x, ctx, wh, wg, wo, gamma, beta, rw, rb, Wu, Wg, Wd, Su, Sg, Sd,
              ident_c, decay_c, before_c, ramp_c, out):
    K = 1024
    xn_dram = nc.dram_tensor("xn_rows", [NT, P, D], F32, kind="Internal").ap()
    xs_dram = nc.dram_tensor("sorted_rows", [(ROUTED + 1) * P, D], F32, kind="Internal").ap()
    ys_dram = nc.dram_tensor("expert_rows", [ROUTED * P, D], F32, kind="Internal").ap()

    room = -(-nc.sbuf_base // 32) * 32

    def sb(name, at, shape, dt=F32):
        return nc.alloc_sbuf_tensor_at(name, [shape[0], int(np.prod(shape[1:]))], dt, offset=room + at)[:, :]

    def view(ap, *dims):
        names = "abcd"[:len(dims)]
        return ap.rearrange(f"p ({' '.join(names)}) -> p {' '.join(names)}", **dict(zip(names, dims)))

    def tensor(name, at, dims, dt=F32, parts=P):
        return view(sb(name, at, [parts, *dims], dt), *dims) if len(dims) > 1 else sb(name, at, [parts, *dims], dt)

    x1 = tensor("x1", 0, [NT, D])
    xhT_hi = tensor("xhT_hi", 0, [C, GW], F32R)
    xhT_lo = tensor("xhT_lo", 8 * K, [C, GW], F32R)
    qT = tensor("qT", 16 * K, [C, GW])
    ctxT = tensor("ctxT", 24 * K, [GT, C, P])
    gate = tensor("gateT", 32 * K, [NG, C, GW])
    x2T = tensor("x2T", 32 * K, [NG, C, GW])
    vals = tensor("values", 64 * K, [C, NT, P])
    wo_hi = tensor("wo_hi", 96 * K, [C, D], F32R)
    wo_lo = tensor("wo_lo", 104 * K, [C, D], F32R)
    wg_hi = tensor("wg_hi", 112 * K, [C, D], F32R)
    wg_lo = tensor("wg_lo", 120 * K, [C, D], F32R)
    sd_hi = tensor("sd_hi", 112 * K, [C, D], F32R)
    sd_lo = tensor("sd_lo", 120 * K, [C, D], F32R)
    su_hi = tensor("su_hi", 128 * K, [C, D], F32R)
    su_lo = tensor("su_lo", 136 * K, [C, D], F32R)
    sg_hi = tensor("sg_hi", 144 * K, [C, D], F32R)
    sg_lo = tensor("sg_lo", 152 * K, [C, D], F32R)
    wh_sb = tensor("wh_sb", 144 * K, [C, P])
    whT = tensor("whT", 146 * K, [C, P])
    gram_hi = tensor("gram_hi", 148 * K, [C, P], F32R)
    gram_lo = tensor("gram_lo", 150 * K, [C, P], F32R)
    decay = tensor("decay", 152 * K, [C, P])
    ring_hi = tensor("ring_hi", 64 * K, [NSLOT, 6, PIECE], F32R)
    xin = tensor("xin", 160 * K, [GT, D])
    cin = tensor("cin", 168 * K, [GT, D])
    zeros = tensor("zeros", 176 * K, [D])
    before_f = tensor("before_f", 178 * K, [P])
    yn = tensor("yn", 160 * K, [GT, D])
    mT_hi = tensor("mT_hi", 168 * K, [C, GW], F32R)
    mT_lo = tensor("mT_lo", 176 * K, [C, GW], F32R)
    ya = tensor("ya", 176 * K, [C, GW])
    HW = GW // 2
    sx_hi = tensor("sx_hi", 160 * K, [C, HW], F32R)
    sx_lo = tensor("sx_lo", 164 * K, [C, HW], F32R)
    shT_hi = tensor("shT_hi", 168 * K, [C, HW], F32R)
    shT_lo = tensor("shT_lo", 172 * K, [C, HW], F32R)
    s_silu = tensor("s_silu", 176 * K, [2, HW])
    s_prod = tensor("s_prod", 178 * K, [2, HW])
    oh = tensor("oh", 180 * K, [TOPK, NT, E])
    expl = tensor("expl", 182 * K, [NT, E])
    rank = tensor("rank", 183 * K, [NT, E])
    tmp = tensor("tmp", 184 * K, [NT, E])
    top8 = tensor("top8", 185 * K, [NT, 8])
    top8i = tensor("top8i", 185 * K + 512, [NT, 8], U32)
    lgT = tensor("lgT", 184 * K, [GW], parts=E)
    raw = tensor("raw", 186 * K, [2, PIECE])
    ident = tensor("ident", 194 * K, [P])
    xn = tensor("xn", 194 * K + 512, [GT, D])
    stage = tensor("stage", 194 * K + 512, [GT, D])
    scores = tensor("scores", 202 * K + 512, [C, P])
    tcmp = tensor("tcmp", 202 * K + 512, [ROUTED, E], BF16, parts=1)
    logits = tensor("logits", 204 * K + 512, [NT, E])
    tab_f = tensor("tab_f", 204 * K + 512, [ROUTED], parts=1)
    tab_e = tensor("tab_e", 204 * K + 704, [ROUTED], I32, parts=1)
    tab_s = tensor("tab_s", 204 * K + 896, [ROUTED], I32, parts=1)
    ends_i = tensor("ends_i", 205 * K + 64, [E], I32, parts=1)
    xs = tensor("xs", 32 * K, [4, D])
    xsT_hi = tensor("xsT_hi", 40 * K, [2, C, P], F32R)
    xsT_lo = tensor("xsT_lo", 44 * K, [2, C, P], F32R)
    r_silu = tensor("r_silu", 48 * K, [2, FE])
    r_prod = tensor("r_prod", 50 * K, [2, FE])
    rhT_hi = tensor("rhT_hi", 52 * K, [2, FC, P], F32R)
    rhT_lo = tensor("rhT_lo", 54 * K, [2, FC, P], F32R)
    yrow = tensor("yrow", 56 * K, [2, D])
    yg = tensor("yg", 64 * K, [GT, TOPK, D])

    top = [205 * K + 512]

    def small(name, dims, dt=F32, parts=P):
        size = 2 if dt == BF16 else 4
        t = tensor(name, top[0], dims, dt, parts)
        top[0] += -(-int(np.prod(dims)) * size // 32) * 32
        return t

    stats = small("stats", [GT, 6])
    mv = small("mv", [GT, 2])
    var_eps = small("var_eps", [GT])
    std = small("std", [GT])
    rstd = small("rstd", [GT])
    nmr = small("nmr", [GT])
    gam_c = small("gam_c", [C])
    bet_c = small("bet_c", [C])
    rwT = small("rwT", [C, E])
    rb_bc = small("rb_bc", [E])
    ramp = small("ramp", [ROUTED + 1])
    before = small("before", [P], BF16)
    ones = small("ones", [P], BF16)
    both = small("both", [NT, E], BF16)
    wts = small("wts", [TOPK, NT])
    pos = small("pos", [TOPK, NT], U32)
    rowv = small("rowv", [NT])
    cnt = small("cnt", [E])
    warm = small("warm", [1])
    tiles_e = small("tiles_e", [E])
    ends = small("ends", [E])
    es = ExitStack()
    with es:
        PS = es.enter_context(nc.psum_tensor("PS", [P, 8, D], F32))

        def sem(name):
            return es.enter_context(nc.semaphore(name))

        early_in, late_in = sem("early_in"), sem("late_in")
        x_in = [sem(f"x_in{b}") for b in range(GT)]
        c_in = [sem(f"c_in{b}") for b in range(GT)]
        again_in = [sem(f"again_in{g}") for g in range(NG)]
        zero_ready, zero_done = sem("zero_ready"), sem("zero_done")
        piece_in = [sem("piece_in0"), sem("piece_in1")]
        expert_in = [sem("expert_in0"), sem("expert_in1")]
        expert_taken = sem("expert_taken")
        pieces = sem("pieces")
        pool_chain = sem("pool_chain")
        whT_full, whT_ready, gram_full, gram_hi_ready, gram_ready = (
            sem(n) for n in ("whT_full", "whT_ready", "gram_full", "gram_hi_ready", "gram_ready"))
        rwT_full, rwT_ready = sem("rwT_full"), sem("rwT_ready")
        var1, std1, xh_ready = sem("var1"), sem("std1"), sem("xh_ready")
        px_full, hi_ready, x_split = sem("px_full"), sem("hi_ready"), sem("x_split")
        pc_full, ctxT_ready = sem("pc_full"), sem("ctxT_ready")
        q_full, q_ready = sem("q_full"), sem("q_ready")
        vw_full, vw_done = sem("vw_full"), sem("vw_done")
        s_full, s_taken, at_ready = sem("s_full"), sem("s_taken"), sem("at_ready")
        o_full, var2, std2, nmr_ready, yn_ready = (
            sem(n) for n in ("o_full", "var2", "std2", "nmr_ready", "yn_ready"))
        py_full, py_done = sem("py_full"), sem("py_done")
        m_ready, mhi_ready, m_split = sem("m_ready"), sem("mhi_ready"), sem("m_split")
        z_full, z_taken = sem("z_full"), sem("z_taken")
        var3, std3, xn_ready = sem("var3"), sem("std3"), sem("xn_ready")
        xn_stored = [sem(f"xn_stored{b}") for b in range(GT)]
        max_sub, exp_ready, both_ready, rank_full, pos_ready, tab_ready = (
            sem(n) for n in ("max_sub", "exp_ready", "both_ready", "rank_full", "pos_ready", "tab_ready"))
        stage_in = [sem(f"stage_in{b}") for b in range(GT)]
        scattered = [sem(f"scattered{b}") for b in range(GT)]
        sxhi_ready, sx_split = sem("sxhi_ready"), sem("sx_split")
        sh_full, ssilu_ready, sprod_ready, shhi_ready, sh_split = (
            sem(n) for n in ("sh_full", "ssilu_ready", "sprod_ready", "shhi_ready", "sh_split"))
        sz_full, sz_taken = sem("sz_full"), sem("sz_taken")
        xs_in = [sem(f"xs_in{b}") for b in range(4)]
        rx_full, rxhi_ready, rx_split = sem("rx_full"), sem("rxhi_ready"), sem("rx_split")
        ug_full, rsilu_ready, rprod_ready = sem("ug_full"), sem("rsilu_ready"), sem("rprod_ready")
        rh_full, rhhi_ready, rh_split = sem("rh_full"), sem("rhhi_ready"), sem("rh_split")
        ry_full, ry_ready = sem("ry_full"), sem("ry_ready")
        y_stored = [sem("y_stored0"), sem("y_stored1")]
        yg_in = [sem(f"yg_in{b}") for b in range(GT)]
        yg_taken, out_ready, out_done = sem("yg_taken"), sem("out_ready"), sem("out_done")
        dve_chain = sem("dve_chain")
        dve_passed, pe_passed, pool_passed = sem("dve_passed"), sem("pe_passed"), sem("pool_passed")

        block = es.enter_context(nc.Block())

        def is_step(g, n):
            return isinstance(g, int) and g == n

        def three(ps, w_hi, w_lo, m_hi, m_lo, start, stop):
            nc.tensor.matmul(ps, w_hi, m_hi, start=start, stop=False)
            nc.tensor.matmul(ps, w_hi, m_lo, start=False, stop=False)
            return nc.tensor.matmul(ps, w_lo, m_hi, start=False, stop=stop)


        @block.sync
        def _(sp):
            x_v = x.rearrange("b p d -> p b d")
            sp.dma_start(ident[:], ident_c).then_inc(early_in, 16)
            sp.dma_start(wh_sb[:], wh.rearrange("h d e -> d h e")).then_inc(early_in, 16)
            for b in range(GT):
                sp.dma_start(xin[:, b, :], x[b]).then_inc(x_in[b], 16)
            for b in range(GT):
                sp.dma_start(cin[:, b, :], ctx[b]).then_inc(c_in[b], 16)
            sp.dma_start(decay[:], decay_c).then_inc(late_in, 16)
            sp.dma_start(before_f[:], before_c).then_inc(late_in, 16)
            sp.dma_start(ramp[:], ramp_c).then_inc(late_in, 16)
            with nc.allow_non_contiguous_dma("columns of two vectors"):
                sp.dma_start(gam_c[:], gamma.rearrange("(c p) -> p c", p=P)).then_inc(late_in, 16)
                sp.dma_start(bet_c[:], beta.rearrange("(c p) -> p c", p=P)).then_inc(late_in, 16)
            sp.dma_start(lgT[:], rw).then_inc(late_in, 16)
            sp.dma_start(rb_bc[:], rb.unsqueeze(0).broadcast_to([P, E])).then_inc(late_in, 16)
            zt = (ROUTED + 1) // (3 * NG)
            xs_zero = xs_dram.rearrange("(n t p) d -> n p t d", p=P, t=zt)
            sp.wait_ge(zero_ready, 1)

            def zero_fill(g):
                for k in range(3):
                    dst = xs_zero[3 * g + k] if isinstance(g, int) else xs_zero[bass.ds(3 * g + k, 1)].squeeze(0)
                    sp.dma_start(dst, zeros[:].unsqueeze(1).broadcast_to([P, zt, D])).then_inc(zero_done, 16)

            zero_fill(0)
            with sp.Fori(1, NG) as g:
                for b in range(GT):
                    sp.wait_ge(px_full, GT * g + (b - GT + 1))
                    sp.dma_start(xin[:, b, :], x[bass.ds(GT * g + b, 1)].squeeze(0)).then_inc(x_in[b], 16)
                for b in range(GT):
                    sp.wait_ge(pc_full, GT * g + (b - GT + 1))
                    sp.dma_start(cin[:, b, :], ctx[bass.ds(GT * g + b, 1)].squeeze(0)).then_inc(c_in[b], 16)
                zero_fill(g)
            sp.wait_ge(vw_full, 2 * GT * NG)
            for g in range(NG):
                sp.dma_start(x1[:, GT * g:GT * g + GT, :], x_v[:, GT * g:GT * g + GT, :]).then_inc(again_in[g], 16)
            with sp.Fori(0, NG) as g:
                for b in range(GT):
                    sp.wait_ge(xn_ready, GT * g + (b + 1))
                    sp.dma_start(xn_dram[bass.ds(GT * g + b, 1)].squeeze(0), xn[:, b, :]).then_inc(xn_stored[b], 16)
            def expert_pieces(e, k0):
                at = (lambda w: w[e]) if isinstance(e, int) else (lambda w: w[bass.ds(e, 1)].squeeze(0))
                srcs = (at(Wu).rearrange("(c p) f -> p c f", p=P), at(Wg).rearrange("(c p) f -> p c f", p=P),
                        at(Wd).rearrange("(c p) f -> p c f", p=P))
                for k, src in enumerate(srcs):
                    slot = (k0 + k) % 2
                    if isinstance(e, int) and 3 * e + k < 2:
                        sp.wait_ge(pieces, 10)
                    else:
                        sp.wait_ge(expert_taken, 3 * e + (k - 1))
                    dst = raw[:, slot, :].rearrange("p (c f) -> p c f", c=src.shape[1])
                    sp.dma_start(dst, src).then_inc(expert_in[slot], 16)

            for e in range(2):
                expert_pieces(e, 3 * e)
            for b in range(GT):
                sp.wait_ge(xn_stored[b], 16 * NG)
            for b in range(GT):
                sp.wait_ge(max_sub, 1)
                sp.dma_start(stage[:, b, :], xn_dram[b]).then_inc(stage_in[b], 16)
            with sp.Fori(1, NG) as g:
                for b in range(GT):
                    sp.wait_ge(scattered[b], 32 * g)
                    sp.dma_start(stage[:, b, :], xn_dram[bass.ds(GT * g + b, 1)].squeeze(0)).then_inc(stage_in[b], 16)
            with sp.Fori(1, E // 2) as e2:
                for h in range(2):
                    expert_pieces(2 * e2 + h, 3 * h)
            with sp.Fori(0, NT) as j:
                sp.wait_ge(out_ready, j + 1)
                sp.dma_start(out[bass.ds(j, 1)].squeeze(0), x1[:, bass.ds(j, 1), :].squeeze(1)).then_inc(out_done, 16)
            sp.wait_ge(out_done, 16 * NT)

        @block.gpsimd
        def _(pool):
            done = [0]

            def split(src, hi, lo):
                nc.gpsimd.tensor_scalar(hi, src, 1.0, 0.0, ALU.mult, ALU.add).then_inc(pool_chain, 1)
                done[0] += 1
                pool.wait_ge(pool_chain, done[0])
                return nc.gpsimd.tensor_tensor(lo, src, hi.bitcast(F32), ALU.subtract)

            static = []
            for w, hi, lo, free in ((wg, wg_hi, wg_lo, None), (wo, wo_hi, wo_lo, None), (Su[0], su_hi, su_lo, None),
                                    (Sg[0], sg_hi, sg_lo, "scores"), (Sd[0], sd_hi, sd_lo, None)):
                for half in range(2):
                    c = 2 * half
                    static.append((w.rearrange("(c p) f -> p c f", p=P)[:, c:c + 2, :], hi[:, c:c + 2, :], lo[:, c:c + 2, :], free))

            def load_static(k):
                pool.dma_start(raw[:, k % 2, :].rearrange("p (c f) -> p c f", c=2), static[k][0]).then_inc(piece_in[k % 2], 16)

            load_static(0)
            load_static(1)
            for k, (_, hi, lo, free) in enumerate(static):
                if k == 6:
                    pool.wait_ge(at_ready, 1)
                    pool.wait_ge(vw_full, 2 * GT * NG)
                pool.wait_ge(piece_in[k % 2], 16 * (k // 2 + 1))
                split(raw[:, k % 2, :].rearrange("p (c f) -> p c f", c=2), hi, lo).then_inc(pieces, 1)
                if k + 2 < len(static):
                    pool.wait_ge(pieces, k + 1)
                    load_static(k + 2)
            n_static = len(static)
            pool.wait_ge(pieces, n_static)

            def expert_piece(slot, k, par, nth):
                pool.wait_ge(expert_in[par], 16 * nth)
                return split(raw[:, par, :], ring_hi[:, slot, k, :], ring_hi[:, slot, 3 + k, :]).then_inc(expert_taken, 1)

            pool.wait_ge(z_full, GT * NG)
            for e in range(2):
                for k in range(3):
                    n = 3 * e + k
                    expert_piece(e % NSLOT, k, n % 2, n // 2 + 1)
            pool.wait_ge(pos_ready, 1)
            pool.wait_ge(zero_done, 16 * 3 * NG)
            for j in range(NT):
                pool.wait_ge(stage_in[j % GT], 16 * (j // GT + 1))
                for k in range(TOPK):
                    nc.gpsimd.indirect_dma_start(xs_dram, bass.IndirectOffsetOnAxis(ap=pos[:, k, j:j + 1], axis=0),
                                                 stage[:, j % GT, :], None).then_inc(scattered[j % GT], 16)
            pool.wait_ge(sz_full, NT)
            for e in range(2, NSLOT):
                for k in range(3):
                    n = 3 * e + k
                    expert_piece(e % NSLOT, k, n % 2, n // 2 + 1)
            pool.wait_ge(tab_ready, 1)
            base = done[0]
            per = 3 * NSLOT
            with pool.Fori(1, E // NSLOT) as r:
                for s in range(NSLOT):
                    last = pool.value_load(ends_i[0:1, bass.ds(NSLOT * r + (s - NSLOT), 1)], min_val=0, max_val=ROUTED)
                    pool.wait_ge(ry_full, last + 1)
                    for k in range(3):
                        n = 3 * s + k
                        pool.wait_ge(expert_in[n % 2], 16 * (per // 2) * r + 16 * (n // 2 + 1))
                        pool.sem_inc(pool_passed, 1)
                        src = raw[:, n % 2, :]
                        hi, lo = ring_hi[:, s, k, :], ring_hi[:, s, 3 + k, :]
                        nc.gpsimd.tensor_scalar(hi, src, 1.0, 0.0, ALU.mult, ALU.add).then_inc(pool_chain, 1)
                        pool.wait_ge(pool_chain, per * r + (n + 1 + base - per))
                        nc.gpsimd.tensor_tensor(lo, src, hi.bitcast(F32), ALU.subtract).then_inc(expert_taken, 1)
            pool.wait_ge(ry_full, ROUTED + 1)
            pool.wait_ge(expert_taken, 3 * E)
            for par in range(2):
                pool.wait_ge(y_stored[par], 16 * ((ROUTED + 1 - par) // 2))
            for j in range(NT):
                if j >= GT:
                    pool.wait_ge(yg_taken, TOPK * (j - GT + 1))
                for k in range(TOPK):
                    nc.gpsimd.indirect_dma_start(yg[:, j % GT, k, :], None, ys_dram,
                                                 bass.IndirectOffsetOnAxis(ap=pos[:, k, j:j + 1], axis=0)).then_inc(yg_in[j % GT], 16)

        @block.scalar
        def _(act):
            for s in (vw_done, py_done):
                act.sem_inc(s, 2)
            act.wait_ge(zero_ready, 1)
            nc.scalar.activation(warm[:], zeros[:, 0:1], ACT.Sqrt)

            def std_of(var_sem, std_sem, n):
                act.wait_ge(var_sem, n)
                nc.scalar.activation(std[:], var_eps[:], ACT.Sqrt).then_inc(std_sem, 1)

            def ctxT_copy(n):
                for b in range(GT):
                    act.wait_ge(pc_full, GT * n + (b + 1))
                    nc.scalar.copy(ctxT[:, b], PS[:, b, :].rearrange("p (c t) -> p c t", c=C)).then_inc(ctxT_ready, 1)

            act.wait_ge(whT_full, 1)
            nc.scalar.copy(whT[:], PS[:, 5, :].rearrange("p (h d) -> p h d", h=C)).then_inc(whT_ready, 1)
            act.wait_ge(gram_full, 1)
            nc.scalar.copy(gram_hi[:], PS[:, 6, :].rearrange("p (h d) -> p h d", h=C)).then_inc(gram_hi_ready, 1)
            std_of(var1, std1, 1)
            ctxT_copy(0)
            act.wait_ge(rwT_full, 1)
            nc.scalar.copy(rwT[:], PS[:, 7, 0:C * E].rearrange("p (c e) -> p c e", c=C)).then_inc(rwT_ready, 1)

            def project(g, last):
                for b in range(GT):
                    act.wait_ge(px_full, GT * g + (b + 1))
                    nc.scalar.copy(xhT_hi[:, :, b * P:(b + 1) * P],
                                   PS[:, b, :].rearrange("p (c t) -> p c t", c=C)).then_inc(hi_ready, 1)
                for b in range(GT):
                    act.wait_ge(vw_full, 2 * GT * g + (b + 1))
                    dst = vals[:, :, GT * g + b, :] if last else vals[:, :, bass.ds(GT * g + b, 1), :].squeeze(2)
                    nc.scalar.copy(dst, PS[:, 5 + b % 2, :].rearrange("p (h d) -> p h d", h=C)).then_inc(vw_done, 1)

                def relu(c):
                    act.wait_ge(vw_full, 2 * GT * g + (GT + c + 1))
                    dst = gate[:, g, c, :] if last else gate[:, bass.ds(g, 1), c, :].squeeze(1)
                    nc.scalar.activation(dst, PS[:, 5 + c % 2, :], ACT.Relu).then_inc(vw_done, 1)

                relu(0)
                relu(1)
                if last:
                    relu(2)
                    std_of(var2, std2, 1)
                    yn_copy(0)
                    relu(3)
                else:
                    ctxT_copy(g + 1)
                    std_of(var1, std1, g + 2)
                    relu(2)
                    relu(3)

            def yn_copy(n):
                act.wait_ge(nmr_ready, n + 1)
                for b in range(GT):
                    nc.scalar.activation(yn[:, b, :].rearrange("p (h d) -> p h d", h=C), PS[:, 0:4, b * P:(b + 1) * P],
                                         ACT.Identity, bias=nmr[:, b:b + 1], scale=rstd[:, b:b + 1]).then_inc(yn_ready, 1)

            def x2_copy(g, o):
                for b in range(GT):
                    act.wait_ge(py_full, o + b + 1)
                    dst = x2T[:, g, :, b * P:(b + 1) * P] if isinstance(g, int) else x2T[:, bass.ds(g, 1), :, b * P:(b + 1) * P].squeeze(1)
                    nc.scalar.copy(dst, PS[:, 4 + b % 2, :].rearrange("p (c t) -> p c t", c=C)).then_inc(py_done, 1)

            def lg_copy(g, o):
                for k in range(2):
                    act.wait_ge(py_full, o + k + 1)
                    j = GT * g + 2 * k
                    dst = logits[:, j:j + 2, :] if isinstance(g, int) else logits[:, bass.ds(j, 2), :]
                    nc.scalar.copy(dst, PS[:, 4 + k, 0:2 * E].rearrange("p (b e) -> p b e", b=2)).then_inc(py_done, 1)

            def attend(g):
                first, last = is_step(g, 0), is_step(g, NG - 1)
                o = 0 if first else 10 * g - 6
                for c in range(C):
                    act.wait_ge(py_full, o + c + 1)
                    nc.scalar.activation(ya[:, c, :], PS[:, 4 + c % 2, :], ACT.Identity,
                                         bias=bet_c[:, c:c + 1], scale=gam_c[:, c:c + 1]).then_inc(py_done, 1)
                for c in range(C):
                    act.wait_ge(m_ready, C * g + (c + 1))
                    src = gate[:, g, c, :] if isinstance(g, int) else gate[:, bass.ds(g, 1), c, :].squeeze(1)
                    nc.scalar.copy(mT_hi[:, c, :], src).then_inc(mhi_ready, 1)
                if not last:
                    std_of(var2, std2, g + 2)
                    yn_copy(g + 1)
                if not first:
                    x2_copy(g - 1, o + 4)
                    lg_copy(g - 1, o + 8)
                if last:
                    act.wait_ge(m_split, C * NG)
                    nc.scalar.copy(sx_hi[:], x2T[:, 0, :, 0:HW]).then_inc(sxhi_ready, 1)
                std_of(var3, std3, g + 1)

            with act.Fori(0, NG - 1) as g:
                project(g, False)
            project(NG - 1, True)
            act.wait_ge(zero_done, 16 * 3 * NG)
            act.wait_ge(at_ready, 1)
            act.wait_ge(late_in, 16 * 7)
            attend(0)
            with act.Fori(1, NG - 1) as g:
                attend(g)
            attend(NG - 1)

            def sx_part(k, g, h):
                act.wait_ge(sh_full, C * k)
                src = x2T[:, g, :, h * HW:(h + 1) * HW] if isinstance(g, int) else x2T[:, bass.ds(g, 1), :, h * HW:(h + 1) * HW].squeeze(1)
                nc.scalar.copy(sx_hi[:], src).then_inc(sxhi_ready, 1)

            def hidden(k):
                def hi(f):
                    act.wait_ge(sprod_ready, C * k + (f + 1 + C))
                    nc.scalar.copy(shT_hi[:, f, :], s_prod[:, f % 2, :]).then_inc(shhi_ready, 1)

                for f in range(C):
                    act.wait_ge(sh_full, C * k + (f + 1))
                    nc.scalar.activation(s_silu[:, f % 2, :], PS[:, f, 0:HW], ACT.Silu).then_inc(ssilu_ready, 1)
                    if f:
                        hi(f - 1)
                hi(C - 1)

            act.wait_ge(z_full, GT * NG)
            hidden(0)
            o = 10 * NG - 6
            x2_copy(NG - 1, o)
            sx_part(1, 0, 1)
            lg_copy(NG - 1, o + 4)
            hidden(1)
            act.wait_ge(py_done, 2 + 10 * NG)
            sx_part(2, 1, 0)
            act.wait_ge(max_sub, 1)
            nc.scalar.activation(expl[:], tmp[:], ACT.Exp).then_inc(exp_ready, 1)
            hidden(2)
            sx_part(3, 1, 1)
            hidden(3)
            with act.Fori(2, NG) as g:
                for h in range(2):
                    sx_part(2 * g + h, g, h)
                    hidden(2 * g + h)

            def load_xs(t, b):
                act.dma_start(xs[:, b, :], xs_dram[bass.ds(t * P, P), :] if not isinstance(t, int) else xs_dram[t * P:(t + 1) * P, :]
                              ).then_inc(xs_in[b], 16)

            def x_hi(n, par):
                act.wait_ge(rx_full, n + 1)
                nc.scalar.copy(xsT_hi[:, par], PS[:, par, :].rearrange("p (c t) -> p c t", c=C)).then_inc(rxhi_ready, 1)

            def silu(n, par):
                act.wait_ge(ug_full, n + 1)
                nc.scalar.activation(r_silu[:, par, :], PS[:, 2 + par, 0:FE], ACT.Silu).then_inc(rsilu_ready, 1)

            def h_hi(n, par):
                act.wait_ge(rh_full, n + 1)
                nc.scalar.copy(rhT_hi[:, par], PS[:, 4, 0:FE].rearrange("p (c t) -> p c t", c=FC)).then_inc(rhhi_ready, 1)

            def y_out(n, par, stored):
                if not isinstance(stored, int) or stored > 0:
                    act.wait_ge(y_stored[par], stored)
                act.wait_ge(ry_full, n + 2)
                nc.scalar.copy(yrow[:, par, :], PS[:, 6 + par, :]).then_inc(ry_ready, 1)
                act.wait_ge(ry_ready, n + 1)
                dst = ys_dram[n * P:(n + 1) * P, :] if isinstance(n, int) else ys_dram[bass.ds(n * P, P), :]
                act.dma_start(dst, yrow[:, par, :]).then_inc(y_stored[par], 16)

            for b in range(GT):
                act.wait_ge(scattered[b], 32 * NG)
            act.wait_ge(sz_full, NT)
            for t in range(4):
                load_xs(t, t)
            x_hi(0, 0)
            x_hi(1, 1)
            silu(0, 0)

            def step(i, k, stored):
                par = k % 2
                if stored is not None:
                    y_out(i - 1, 1 - par, stored)
                x_hi(i + 2, par)
                if not isinstance(i, int) or i + 4 <= ROUTED:
                    load_xs(i + 4, k)
                h_hi(i, par)
                silu(i + 1, 1 - par)

            for i in range(4):
                step(i, i, None if i == 0 else 16 * ((i - 1) // 2))
            last = (ROUTED - 3) // 4
            with act.Fori(1, last) as q:
                for k in range(4):
                    step(4 * q + k, k, 32 * q + 16 * ((k - 1) // 2))
            for i in range(4 * last, ROUTED - 1):
                step(i, i % 4, 16 * ((i - 1) // 2))
            i = ROUTED - 1
            y_out(i - 1, (i - 1) % 2, 16 * ((i - 1) // 2))
            h_hi(i, i % 2)
            y_out(i, i % 2, 16 * (i // 2))

        @block.vector
        def _(dve):
            ticks = [0]

            def pass_on():
                dve.sem_inc(dve_passed, 1)

            def link(ins, plain=False):
                ticks[0] = ticks[0] + 1
                ins.then_inc(dve_chain, 1)
                dve.wait_ge(dve_chain, ticks[0])
                if plain:
                    pass_on()

            for s in (z_taken, sh_split, rx_split, sz_taken):
                dve.sem_inc(s, 2)
            dve.sem_inc(sprod_ready, C)
            for s in (q_ready, s_taken, rh_split):
                dve.sem_inc(s, 1)
            nc.vector.memset(zeros[:], 0.0).then_inc(zero_ready, 1)
            nc.vector.memset(ones[:], 1.0)
            link(nc.vector.memset(scores[:], 0.0))
            def normal(srcs, eps, var_sem, std_sem, n, n_std):
                for b, src in enumerate(srcs):
                    i = nc.vector.bn_stats(stats[:, b, :], src)
                link(i, plain=True)
                for b in range(GT):
                    i = nc.vector.bn_aggr(mv[:, b, :], stats[:, b, :])
                link(i)
                nc.vector.tensor_scalar(var_eps[:], mv[:, :, 1], eps, None, ALU.add).then_inc(var_sem, 1)
                dve.wait_ge(std_sem, n_std)
                return nc.vector.reciprocal(rstd[:], std[:])

            def normal_x(n):
                for b in range(GT):
                    dve.wait_ge(x_in[b], 16 * n + 16)
                link(normal([xin[:, b, :] for b in range(GT)], LN_EPS, var1, std1, n, n + 1))
                for b in range(GT):
                    nc.vector.tensor_scalar(xin[:, b, :], xin[:, b, :], mv[:, b, 0:1], rstd[:, b:b + 1],
                                            ALU.subtract, ALU.mult).then_inc(xh_ready, 1)

            normal_x(0)
            dve.wait_ge(gram_hi_ready, 1)
            nc.vector.tensor_tensor(gram_lo[:], PS[:, 6, :].rearrange("p (h d) -> p h d", h=C),
                                    gram_hi[:].bitcast(F32), ALU.subtract).then_inc(gram_ready, 1)

            def project(g):
                for b in range(GT):
                    dve.wait_ge(hi_ready, GT * g + (b + 1))
                    nc.vector.tensor_tensor(xhT_lo[:, :, b * P:(b + 1) * P], PS[:, b, :].rearrange("p (c t) -> p c t", c=C),
                                            xhT_hi[:, :, b * P:(b + 1) * P].bitcast(F32), ALU.subtract).then_inc(x_split, 1)
                for h in range(C):
                    dve.wait_ge(q_full, C * g + (h + 1))
                    nc.vector.tensor_copy(qT[:, h, :], PS[:, 4, :]).then_inc(q_ready, 1)
                dve.wait_ge(s_full, g + 1)
                nc.vector.tensor_tensor(scores[:], PS[:, 7, :].rearrange("p (h s) -> p h s", h=C), scores[:],
                                        ALU.add).then_inc(s_taken, 1)
                dve.wait_ge(s_taken, g + 2)

            base = ticks[0]
            per = 4
            with dve.Fori(0, NG - 1) as g:
                ticks[0] = per * g + base
                project(g)
                link(nc.vector.tensor_copy(rowv[:, 0:1], scores[:, 0, 0:1]))
                normal_x(g + 1)
            ticks[0] = base + per * (NG - 1)
            project(NG - 1)
            dve.wait_ge(late_in, 16 * 7)
            nc.vector.tensor_copy(before[:], before_f[:])
            link(nc.vector.tensor_tensor(scores[:], scores[:], decay[:], ALU.mult))
            link(nc.vector.scalar_tensor_tensor(scores[:], scores[:], -1.0, scores[:], ALU.mult, ALU.max))
            nc.vector.tensor_scalar(scores[:], scores[:], 1.0, None, ALU.max).then_inc(at_ready, 1)

            def normal_o(n):
                dve.wait_ge(o_full, n + 1)
                link(normal([PS[:, 0:4, b * P:(b + 1) * P] for b in range(GT)], GN_EPS, var2, std2, n, n + 1))
                nc.vector.scalar_tensor_tensor(nmr[:], mv[:, :, 0], -1.0, rstd[:], ALU.mult, ALU.mult).then_inc(nmr_ready, 1)

            def attend(g):
                first, last = is_step(g, 0), is_step(g, NG - 1)
                still = isinstance(g, int)
                gt = [gate[:, g, c, :] if still else gate[:, bass.ds(g, 1), c, :].squeeze(1) for c in range(C)]
                o = 2 + (0 if first else 10 * g - 6)

                def lo(c):
                    dve.wait_ge(mhi_ready, C * g + (c + 1))
                    nc.vector.tensor_tensor(mT_lo[:, c, :], gt[c], mT_hi[:, c, :].bitcast(F32), ALU.subtract).then_inc(m_split, 1)

                for c in range(C):
                    dve.wait_ge(py_done, o + (c + 1))
                    nc.vector.tensor_tensor(gt[c], ya[:, c, :], gt[c], ALU.mult).then_inc(m_ready, 1)
                for c in range(C):
                    lo(c)
                if not last:
                    normal_o(g + 1)
                if first:
                    for k in range(NG):
                        dve.wait_ge(again_in[k], 16)
                rows = [x1[:, GT * g + b, :] if still else x1[:, bass.ds(GT * g + b, 1), :].squeeze(1) for b in range(GT)]
                for b in range(GT):
                    if last and b == GT - 1:
                        sx_rest(0, 0, 0)
                    dve.wait_ge(z_full, GT * g + (b + 1))
                    nc.vector.tensor_tensor(rows[b], PS[:, 6 + b % 2, :], rows[b], ALU.add).then_inc(z_taken, 1)
                dve.wait_ge(z_taken, GT * g + (GT + 2))
                pass_on()
                link(normal(rows, LN_EPS, var3, std3, g, g + 1))
                for b in range(GT):
                    if not first:
                        dve.wait_ge(xn_stored[b], 16 * g)
                        dve.wait_ge(py_full, 10 * g - 2 + (b + 1))
                    nc.vector.tensor_scalar(xn[:, b, :], rows[b], mv[:, b, 0:1], rstd[:, b:b + 1],
                                            ALU.subtract, ALU.mult).then_inc(xn_ready, 1)

            def sx_rest(k, g, h):
                src = x2T[:, g, :, h * HW:(h + 1) * HW] if isinstance(g, int) else x2T[:, bass.ds(g, 1), :, h * HW:(h + 1) * HW].squeeze(1)
                dve.wait_ge(sxhi_ready, k + 1)
                nc.vector.tensor_tensor(sx_lo[:], src, sx_hi[:].bitcast(F32), ALU.subtract).then_inc(sx_split, 1)

            def hidden(k):
                def lo(f):
                    dve.wait_ge(shhi_ready, C * k + (f + 1))
                    nc.vector.tensor_tensor(shT_lo[:, f, :], s_prod[:, f % 2, :], shT_hi[:, f, :].bitcast(F32),
                                            ALU.subtract).then_inc(sh_split, 1)

                for f in range(C):
                    dve.wait_ge(ssilu_ready, C * k + (f + 1))
                    dve.wait_ge(sh_split, C * k + (f + 1))
                    nc.vector.tensor_tensor(s_prod[:, f % 2, :], PS[:, f, HW:2 * HW], s_silu[:, f % 2, :], ALU.mult).then_inc(sprod_ready, 1)
                    if f:
                        lo(f - 1)
                lo(C - 1)

            def add_shared(k, g, h):
                for b in range(2):
                    dve.wait_ge(sz_full, 2 * k + (b + 1))
                    j = GT * g + (2 * h + b)
                    row = x1[:, j, :] if isinstance(g, int) else x1[:, bass.ds(j, 1), :].squeeze(1)
                    nc.vector.tensor_tensor(row, PS[:, 6 + b, :], row, ALU.add).then_inc(sz_taken, 1)

            normal_o(0)
            dve.wait_ge(zero_done, 16 * 3 * NG)
            attend(0)
            base = ticks[0]
            per = 6
            with dve.Fori(1, NG - 1) as g:
                ticks[0] = per * g + (base - per)
                attend(g)
            ticks[0] = base + per * (NG - 2)
            attend(NG - 1)
            hidden(0)
            sx_rest(1, 0, 1)
            add_shared(0, 0, 0)

            def bc_t(v):
                return v.unsqueeze(1).broadcast_to([P, NT, E])

            def bc_e(v):
                return v.unsqueeze(2).broadcast_to([P, NT, E])

            dve.wait_ge(py_done, 2 + 10 * NG)
            nc.vector.tensor_reduce(rowv[:], logits[:], AX.X, ALU.max)
            link(nc.vector.tensor_tensor(rank[:], logits[:], bc_t(rb_bc[:]), ALU.add))
            nc.vector.tensor_tensor(tmp[:], logits[:], bc_e(rowv[:]), ALU.subtract).then_inc(max_sub, 1)
            for j in range(NT):
                ins = nc.vector.max(top8[:, j, :], rank[:, j, :])
            link(ins)
            for j in range(NT):
                ins = nc.vector.max_index(top8i[:, j, :], top8[:, j, :], rank[:, j, :])
            link(ins)
            for k in range(TOPK):
                link(nc.vector.tensor_copy(rowv[:], top8i[:, :, k]))
                link(nc.vector.tensor_tensor(oh[:, k], bc_t(ramp[:, 0:E]), bc_e(rowv[:]), ALU.is_equal))
            nc.vector.tensor_tensor(both[:], oh[:, 0], oh[:, 1], ALU.add).then_inc(both_ready, 1)
            hidden(1)
            sx_rest(2, 1, 0)
            add_shared(1, 0, 1)
            dve.wait_ge(exp_ready, 1)
            for k in range(TOPK):
                link(nc.vector.tensor_tensor(tmp[:], oh[:, k], expl[:], ALU.mult))
                link(nc.vector.tensor_reduce(wts[:, k, :], tmp[:], AX.X, ALU.add))
            link(nc.vector.tensor_tensor(rowv[:], wts[:, 0, :], wts[:, 1, :], ALU.add))
            link(nc.vector.reciprocal(rowv[:], rowv[:]))
            for k in range(TOPK):
                nc.vector.tensor_tensor(wts[:, k, :], wts[:, k, :], rowv[:], ALU.mult)
            dve.wait_ge(rank_full, 1)
            link(nc.vector.tensor_scalar(cnt[:], PS[:, 4, NT * E:NT * E + E], 1.0, None, ALU.max))
            link(nc.vector.tensor_scalar(tmp[:], bc_e(ramp[:, 0:NT]), float(P), None, ALU.mult))
            link(nc.vector.tensor_tensor(tmp[:], bc_t(cnt[:]), tmp[:], ALU.is_gt))
            link(nc.vector.tensor_reduce(tiles_e[:], tmp[:].rearrange("p k e -> p e k"), AX.X, ALU.add))
            link(nc.vector.tensor_tensor_scan(ends[:], tiles_e[:], tiles_e[:], 0.0, ALU.add, ALU.bypass))
            link(nc.vector.tensor_tensor(tiles_e[:], ends[:], tiles_e[:], ALU.subtract))
            link(nc.vector.tensor_scalar(tiles_e[:], tiles_e[:], float(P), None, ALU.mult))
            link(nc.vector.tensor_tensor(rank[:], PS[:, 4, 0:NT * E].rearrange("p (t e) -> p t e", t=NT), bc_t(tiles_e[:]), ALU.add))
            for k in range(TOPK):
                link(nc.vector.tensor_tensor(tmp[:], oh[:, k], rank[:], ALU.mult))
                link(nc.vector.tensor_reduce(rowv[:], tmp[:], AX.X, ALU.add))
                ins = nc.vector.tensor_copy(pos[:, k, :], rowv[:])
                if k < TOPK - 1:
                    link(ins)
            ins.then_inc(pos_ready, 1)
            nc.vector.tensor_copy(ends_i[:], ends[0:1, :])
            link(nc.vector.tensor_tensor(tcmp[:], ends[0:1, :].unsqueeze(1).broadcast_to([1, ROUTED, E]),
                                         ramp[0:1, 0:ROUTED].unsqueeze(2).broadcast_to([1, ROUTED, E]), ALU.is_le))
            link(nc.vector.tensor_reduce(tab_f[:], tcmp[:], AX.X, ALU.add))
            link(nc.vector.tensor_scalar(tab_f[:], tab_f[:], float(E - 1), None, ALU.min))
            link(nc.vector.tensor_copy(tab_e[:], tab_f[:]))
            nc.vector.tensor_scalar(tab_s[:], tab_e[:], NSLOT - 1, None, ALU.bitwise_and).then_inc(tab_ready, 1)

            hidden(2)
            sx_rest(3, 1, 1)
            add_shared(2, 1, 0)
            hidden(3)
            add_shared(3, 1, 1)
            with dve.Fori(2, NG) as g:
                for h in range(2):
                    sx_rest(2 * g + h, g, h)
                    hidden(2 * g + h)
                    add_shared(2 * g + h, g, h)

            def x_lo(n, par):
                dve.wait_ge(rxhi_ready, n + 1)
                nc.vector.tensor_tensor(xsT_lo[:, par], PS[:, par, :].rearrange("p (c t) -> p c t", c=C),
                                        xsT_hi[:, par].bitcast(F32), ALU.subtract).then_inc(rx_split, 1)

            def prod(n, par):
                dve.wait_ge(rsilu_ready, n + 1)
                nc.vector.tensor_tensor(r_prod[:, par, :], PS[:, 2 + par, FE:2 * FE], r_silu[:, par, :], ALU.mult).then_inc(rprod_ready, 1)

            def h_lo(n, par):
                dve.wait_ge(rhhi_ready, n + 1)
                nc.vector.tensor_tensor(rhT_lo[:, par], PS[:, 4, 0:FE].rearrange("p (c t) -> p c t", c=FC),
                                        rhT_hi[:, par].bitcast(F32), ALU.subtract).then_inc(rh_split, 1)

            x_lo(0, 0)
            x_lo(1, 1)
            prod(0, 0)
            with dve.Fori(0, (ROUTED - 1) // 2) as q:
                for par in range(2):
                    i = 2 * q + par
                    x_lo(i + 2, par)
                    h_lo(i, par)
                    prod(i + 1, 1 - par)
            h_lo(ROUTED - 1, (ROUTED - 1) % 2)

            dve.wait_ge(sz_taken, NT + 2)
            with dve.Fori(0, NG) as g:
                for b in range(GT):
                    dve.wait_ge(yg_in[b], 32 * g + 32)
                    row = x1[:, bass.ds(GT * g + b, 1), :].squeeze(1)
                    for k in range(TOPK):
                        ins = nc.vector.scalar_tensor_tensor(row, yg[:, b, k, :], wts[:, k, bass.ds(GT * g + b, 1)], row, ALU.mult, ALU.add)
                        if k == 0:
                            ins.then_inc(yg_taken, 1)
                            dve.wait_ge(yg_taken, 2 * GT * g + (2 * b + 1))
                    ins.then_inc(yg_taken, 1)
                    dve.wait_ge(yg_taken, 2 * GT * g + (2 * b + 2))
                    dve.sem_inc(out_ready, 1)

        @block.tensor
        def _(pe):
            def transposes(bank, srcs, width=P):
                for c, s in enumerate(srcs):
                    ins = nc.tensor.transpose(PS[:, bank, c * width:(c + 1) * width], s, ident[0:s.shape[0], 0:s.shape[0]])
                return ins

            pe.sem_inc(ry_full, 1)

            def ctx_transposes(n):
                for b in range(GT):
                    pe.wait_ge(c_in[b], 16 * n + 16)
                    if not is_step(n, 0):
                        pe.wait_ge(x_split, GT * n + (b + 1 - GT))
                    transposes(b, [cin[:, b, c * P:(c + 1) * P] for c in range(C)]).then_inc(pc_full, 1)

            pe.wait_ge(early_in, 32)
            transposes(5, [wh_sb[:, h, :] for h in range(C)]).then_inc(whT_full, 1)
            pe.wait_ge(whT_ready, 1)
            for h in range(C):
                ins = nc.tensor.matmul(PS[:, 6, h * P:(h + 1) * P], whT[:, h, :], whT[:, h, :], start=True, stop=True)
            ins.then_inc(gram_full, 1)
            ctx_transposes(0)
            pe.wait_ge(late_in, 16 * 7)
            transposes(7, [lgT[:, c * P:(c + 1) * P] for c in range(C)], E).then_inc(rwT_full, 1)
            pe.wait_ge(gram_ready, 1)
            pe.wait_ge(rwT_ready, 1)

            def project(g, last):
                for b in range(GT):
                    pe.wait_ge(xh_ready, GT * g + (b + 1))
                    pe.wait_ge(ctxT_ready, GT * g + (b + 1))
                    transposes(b, [xin[:, b, c * P:(c + 1) * P] for c in range(C)]).then_inc(px_full, 1)

                def q_mm(h):
                    pe.wait_ge(q_ready, C * g + (h + 1))
                    three(PS[:, 4, :], gram_hi[:, h, :], gram_lo[:, h, :], xhT_hi[:, h, :], xhT_lo[:, h, :],
                          True, True).then_inc(q_full, 1)

                def s_mm(h):
                    pe.wait_ge(q_ready, C * g + (h + 2))
                    if h == 0:
                        pe.wait_ge(s_taken, g + 1)
                    for b in range(GT):
                        ins = nc.tensor.matmul(PS[:, 7, h * P:(h + 1) * P], ctxT[:, b, h, :], qT[:, h, b * P:(b + 1) * P],
                                               start=(b == 0), stop=(b == GT - 1))
                    if h == C - 1:
                        ins.then_inc(s_full, 1)

                def v_mm(b):
                    pe.wait_ge(vw_done, 2 * GT * g + (b + 1))
                    for h in range(C):
                        ins = nc.tensor.matmul(PS[:, 5 + b % 2, h * P:(h + 1) * P], ctxT[:, b, h, :], wh_sb[:, h, :],
                                               start=True, stop=True)
                    ins.then_inc(vw_full, 1)

                def gate_mm(o):
                    pe.wait_ge(vw_done, 2 * GT * g + (GT + o + 1))
                    for c in range(C):
                        ins = three(PS[:, 5 + o % 2, :], wg_hi[:, c, o * P:(o + 1) * P], wg_lo[:, c, o * P:(o + 1) * P],
                                    xhT_hi[:, c, :], xhT_lo[:, c, :], c == 0, c == C - 1)
                    ins.then_inc(vw_full, 1)

                v_mm(0)
                v_mm(1)
                pe.wait_ge(x_split, GT * g + GT)
                q_mm(0)
                v_mm(2)
                q_mm(1)
                s_mm(0)
                v_mm(3)
                q_mm(2)
                s_mm(1)
                pe.wait_ge(pieces, 2)
                q_mm(3)
                s_mm(2)
                gate_mm(0)
                s_mm(3)
                gate_mm(1)
                if last:
                    values_mm(0)
                else:
                    ctx_transposes(g + 1)
                gate_mm(2)
                gate_mm(3)

            def values_mm(n):
                if is_step(n, 0):
                    pe.wait_ge(at_ready, 1)
                    pe.wait_ge(vw_done, 2 * GT * NG - C + 2)
                for h in range(C):
                    v = vals[:, h, GT * n:GT * n + GT, :] if isinstance(n, int) else vals[:, h, bass.ds(GT * n, GT), :]
                    ins = nc.tensor.matmul(PS[:, h, :].rearrange("p (b d) -> p b d", b=GT), scores[:, h, :], v, start=True, stop=True)
                ins.then_inc(o_full, 1)

            def x2_transposes(g, o):
                for b in range(GT):
                    pe.wait_ge(xn_ready, GT * g + (b + 1))
                    pe.wait_ge(py_done, o + (b + 1))
                    transposes(4 + b % 2, [xn[:, b, c * P:(c + 1) * P] for c in range(C)]).then_inc(py_full, 1)

            def logits_mm(g, o):
                pe.wait_ge(py_done, o + 2)
                for k in range(2):
                    for b in range(2):
                        t = (2 * k + b) * P
                        for c in range(C):
                            ins = nc.tensor.matmul(PS[:, 4 + k, b * E:(b + 1) * E], x2T[:, g, c, t:t + P], rwT[:, c, :], start=(c == 0), stop=(c == C - 1))
                    ins.then_inc(py_full, 1)

            def attend(g):
                first, last = is_step(g, 0), is_step(g, NG - 1)
                o = 0 if first else 10 * g - 6
                pe.wait_ge(yn_ready, GT * g + GT)
                for c in range(C):
                    pe.wait_ge(py_done, o + (c + 1))
                    transposes(4 + c % 2, [yn[:, b, c * P:(c + 1) * P] for b in range(GT)]).then_inc(py_full, 1)
                if not last:
                    values_mm(g + 1)

                def out_mm(b):
                    pe.wait_ge(z_taken, GT * g + (b + 1))
                    for c in range(C):
                        ins = three(PS[:, 6 + b % 2, :], mT_hi[:, c, b * P:(b + 1) * P], mT_lo[:, c, b * P:(b + 1) * P],
                                    wo_hi[:, c, :], wo_lo[:, c, :], c == 0, c == C - 1)
                    ins.then_inc(z_full, 1)

                pe.wait_ge(m_split, C * g + C)
                out_mm(0)
                out_mm(1)
                if not first:
                    x2_transposes(g - 1, o + 4)
                out_mm(2)
                if not first:
                    logits_mm(g - 1, o + 8)
                out_mm(3)

            with pe.Fori(0, NG - 1) as g:
                project(g, False)
            project(NG - 1, True)
            pe.wait_ge(pieces, 4)
            pe.wait_ge(vw_done, 2 + 2 * GT * NG)
            for g in range(NG):
                attend(g)

            def ranks():
                pe.wait_ge(both_ready, 1)
                R = PS[:, 4, 0:NT * E].rearrange("p (t e) -> p t e", t=NT)
                nc.tensor.matmul(R, before[:], both[:], start=True, stop=False)
                for t in range(NT - 1):
                    nc.tensor.matmul(R[:, t + 1:NT, :], ones[:], both[:, t:t + 1, :].broadcast_to([P, NT - 1 - t, E]),
                                     start=False, stop=(t == NT - 2))
                for t in range(NT):
                    ins = nc.tensor.matmul(PS[:, 4, NT * E:NT * E + E], ones[:], both[:, t, :], start=(t == 0), stop=(t == NT - 1))
                ins.then_inc(rank_full, 1)

            def shared_up(k):
                pe.wait_ge(sx_split, k + 1)
                for f in range(C):
                    pe.wait_ge(sprod_ready, C * k + (f + 1))
                    for part, (w_hi, w_lo) in enumerate(((su_hi, su_lo), (sg_hi, sg_lo))):
                        for c in range(C):
                            ins = three(PS[:, f, part * HW:(part + 1) * HW], w_hi[:, c, f * P:(f + 1) * P],
                                        w_lo[:, c, f * P:(f + 1) * P], sx_hi[:, c, :], sx_lo[:, c, :], c == 0, c == C - 1)
                    ins.then_inc(sh_full, 1)

            def shared_down(k):
                pe.wait_ge(sz_taken, 2 * k + 2)
                for f in range(C):
                    pe.wait_ge(sh_split, C * k + (f + 3))
                    for b in range(2):
                        ins = three(PS[:, 6 + b, :], shT_hi[:, f, b * P:(b + 1) * P], shT_lo[:, f, b * P:(b + 1) * P],
                                    sd_hi[:, f, :], sd_lo[:, f, :], f == 0, f == C - 1)
                        if f == C - 1:
                            ins.then_inc(sz_full, 1)

            pe.wait_ge(pieces, 10)
            shared_up(0)
            o = 10 * NG - 6
            x2_transposes(NG - 1, o)
            pe.wait_ge(z_taken, GT * NG + 2)
            shared_down(0)
            logits_mm(NG - 1, o + 4)
            shared_up(1)
            ranks()
            shared_down(1)
            for k in range(2, 4):
                shared_up(k)
                shared_down(k)
            with pe.Fori(2, NG) as g:
                for h in range(2):
                    shared_up(2 * g + h)
                    shared_down(2 * g + h)

            def x_turn(n, par, b, loads):
                pe.wait_ge(xs_in[b], loads)
                pe.wait_ge(rx_split, n + 1)
                transposes(par, [xs[:, b, c * P:(c + 1) * P] for c in range(C)]).then_inc(rx_full, 1)

            def up(n, par, e, slot):
                pe.wait_ge(expert_taken, 3 * e + 3)
                pe.wait_ge(rx_split, n + 3)
                W = ring_hi[:, bass.ds(slot, 1), :, :].squeeze(1)
                ps = PS[:, 2 + par, :].rearrange("p (a f) -> p a f", a=2)
                for c in range(C):
                    hi = W[:, 0:2, c * FE:(c + 1) * FE]
                    lo = W[:, 3:5, c * FE:(c + 1) * FE]
                    ins = three(ps, xsT_hi[:, par, c, :], xsT_lo[:, par, c, :], hi, lo, c == 0, c == C - 1)
                ins.then_inc(ug_full, 1)

            def h_turn(n, par):
                pe.wait_ge(rprod_ready, n + 1)
                pe.wait_ge(rh_split, n + 1)
                transposes(4, [r_prod[:, par, c * P:(c + 1) * P] for c in range(FC)]).then_inc(rh_full, 1)

            def down(n, par, slot):
                pe.wait_ge(rh_split, n + 2)
                W = ring_hi[:, bass.ds(slot, 1), :, :].squeeze(1)
                for f in range(FC):
                    ins = three(PS[:, 6 + par, :], rhT_hi[:, par, f, :], rhT_lo[:, par, f, :],
                                W[:, 2, f * D:(f + 1) * D], W[:, 5, f * D:(f + 1) * D], f == 0, f == FC - 1)
                ins.then_inc(ry_full, 1)

            def tile_expert(n):
                return pe.value_load(tab_e[0:1, bass.ds(n, 1)], min_val=0, max_val=E - 1)

            def tile_slot(n):
                return pe.value_load(tab_s[0:1, bass.ds(n, 1)], min_val=0, max_val=NSLOT - 1)

            def step(i, par, b, loads):
                e = tile_expert(i + 1)
                x_turn(i + 2, par, b, loads)
                slot = tile_slot(i + 1)
                h_turn(i, par)
                up(i + 1, 1 - par, e, slot)
                old = tile_slot(i)
                if not isinstance(i, int) or i >= 2:
                    pe.wait_ge(ry_ready, i - 1)
                down(i, par, old)

            pe.wait_ge(tab_ready, 1)
            pe.wait_ge(sz_taken, NT + 2)
            x_turn(0, 0, 0, 16)
            x_turn(1, 1, 1, 16)
            up(0, 0, tile_expert(0), tile_slot(0))
            step(0, 0, 2, 16)
            step(1, 1, 3, 16)
            n_full = (ROUTED - 1 - 2) // 4
            with pe.Fori(0, n_full) as q:
                for k in range(4):
                    step(4 * q + (2 + k), k % 2, k, 16 * q + 32)
            for i in range(2 + 4 * n_full, ROUTED - 1):
                step(i, i % 2, (i + 2) % 4, 16 * ((i + 2) // 4 + 1))
            i = ROUTED - 1
            h_turn(i, i % 2)
            pe.wait_ge(ry_ready, i - 1)
            down(i, i % 2, tile_slot(i))


_INS = {"x": "x", "ctx_2048": "ctx", "L0_xattn_Wh": "wh", "L0_xattn_wg_w": "wg", "L0_xattn_wo_w": "wo",
        "L0_xattn_gn_gamma": "gamma", "L0_xattn_gn_beta": "beta", "L0_ffn_router_w": "rw",
        "L0_ffn_router_bias": "rb", "L0_ffn_Wu": "Wu", "L0_ffn_Wg": "Wg", "L0_ffn_Wd": "Wd",
        "L0_ffn_Su": "Su", "L0_ffn_Sg": "Sg", "L0_ffn_Sd": "Sd"}


def shape_constants():
    return {
        "ident_c": np.eye(P, dtype=np.float32),
        "decay_c": decay_over_root(C, P, P),
        "before_c": np.triu(np.ones((P, P), np.float32), 1),
        "ramp_c": np.tile(np.arange(ROUTED + 1, dtype=np.float32), (P, 1)),
    }


def kernel(**inputs):
    import concourse.bacc as bacc
    from concourse.bass_utils import run_bass_kernel_spmd

    nc = bacc.Bacc("TRN2", target_bir_lowering=False, num_devices=1)
    arrays, args = {}, {}
    for name, arg in _INS.items():
        arrays[f"in_{arg}"] = np.ascontiguousarray(inputs[name])
    for arg, a in shape_constants().items():
        arrays[f"in_{arg}"] = a
    for name, a in arrays.items():
        args[name[3:]] = nc.dram_tensor(name, a.shape, mybir.dt.from_np(a.dtype), kind="ExternalInput").ap()
    out = nc.dram_tensor("out_rows", (NT, P, D), F32, kind="ExternalOutput").ap()
    xattn_moe(nc, **args, out=out)
    r = run_bass_kernel_spmd(nc, [arrays], core_ids=[0])
    return r.results[0]["out_rows"]
```
